# Optimizing a Trainium2 kernel written in Bass

```python
import numpy as np
import jax
import jax.numpy as jnp

def _softmax(x, axis=-1):
    return jax.nn.softmax(x, axis=axis)

def _gelu(x):
    return jax.nn.gelu(x, approximate=True)

def _silu(x):
    return jax.nn.silu(x)

def _sigmoid(x):
    return jax.nn.sigmoid(x)

def _layernorm(x, axis=-1, eps=1e-05):
    m = jnp.mean(x, axis=axis, keepdims=True)
    v = jnp.var(x, axis=axis, keepdims=True)
    return (x - m) / jnp.sqrt(v + eps)

def _scatter_add(tgt, idx, src, axis=0):
    return tgt.at[idx].add(src)

def _segment_sum(src, seg, n):
    return jax.ops.segment_sum(src, seg, n)
kernel_name = 'mk_vit_tower_d4_tok_img256_r4_88068c'

def setup_inputs(seed: int=0):
    np.random.seed(seed)
    _w = jnp.asarray

    def _rec_inputs():
        import jax
        import jax.numpy as jnp
        _rk = jax.random.key(seed)
        x = -0.000928989 + 1.00043 * jax.random.normal(jax.random.fold_in(_rk, 1), (128, 64, 64, 1), jnp.float32)
        return x
    x = _rec_inputs()

    def _L0_tok_setup():
        import jax, jax.numpy as jnp
        import numpy as np
        B, S, D_A, D_V, D_U, L, M1, M2 = (16, 64, 3, 32, 1, 4, 12, 12)
        MID = 4 * D_U

        def conv1x1(x, w, b):
            return jnp.einsum('bixy,oi->boxy', x, w) + b[None, :, None, None]

        def fourier_layer(x, fw_i):
            Bm, C, M, N = x.shape
            x_ft = jnp.fft.rfft2(x, s=(M, N), norm='ortho')
            w_lo = fw_i[0, ..., 0] + 1j * fw_i[0, ..., 1]
            w_hi = fw_i[1, ..., 0] + 1j * fw_i[1, ..., 1]
            lo = jnp.einsum('bixy,ioxy->boxy', x_ft[:, :, :M1, :M2], w_lo)
            hi = jnp.einsum('bixy,ioxy->boxy', x_ft[:, :, -M1:, :M2], w_hi)
            out_ft = jnp.zeros(x_ft.shape, dtype=x_ft.dtype)
            out_ft = out_ft.at[:, :, :M1, :M2].set(lo)
            out_ft = out_ft.at[:, :, -M1:, :M2].set(hi)
            return jnp.fft.irfft2(out_ft, s=(M, N), norm='ortho')

        def make_grid(b, sx, sy):
            gx = jnp.broadcast_to(jnp.linspace(0.0, 1.0, sx)[None, :, None], (b, sx, sy))
            gy = jnp.broadcast_to(jnp.linspace(0.0, 1.0, sy)[None, None, :], (b, sx, sy))
            return jnp.stack([gx, gy], axis=-1)
        key = jax.random.key(seed)
        ks = jax.random.split(key, 12)
        sc_v = 1.0 / np.sqrt(D_V)
        inp = {'x': jax.random.normal(ks[0], (B, S, S, D_A - 2), dtype=jnp.float32), 'p_w': jax.random.normal(ks[1], (D_V, D_A), dtype=jnp.float32) / np.sqrt(D_A), 'p_b': jnp.zeros((D_V,), dtype=jnp.float32), 'fw': jax.random.normal(ks[2], (L, 2, D_V, D_V, M1, M2, 2), dtype=jnp.float32) * sc_v, 'w1_w': jax.random.normal(ks[3], (L, D_V, D_V), dtype=jnp.float32) * sc_v, 'w1_b': jnp.zeros((L, D_V), dtype=jnp.float32), 'w2_w': jax.random.normal(ks[4], (L, D_V, D_V), dtype=jnp.float32) * sc_v, 'w2_b': jnp.zeros((L, D_V), dtype=jnp.float32), 'q1_w': jax.random.normal(ks[5], (MID, D_V), dtype=jnp.float32) * sc_v, 'q1_b': jnp.zeros((MID,), dtype=jnp.float32), 'q2_w': jax.random.normal(ks[6], (D_U, MID), dtype=jnp.float32) / np.sqrt(MID), 'q2_b': jnp.zeros((D_U,), dtype=jnp.float32)}
        return inp
    _L0_tok_all = _L0_tok_setup()
    _L0_tok_in = {k: v for k, v in _L0_tok_all.items() if k in ('p_w', 'p_b', 'fw', 'w1_w', 'w1_b', 'w2_w', 'w2_b', 'q1_w', 'q1_b', 'q2_w', 'q2_b')}
    del _L0_tok_all

    def _L0_attn_setup():
        import jax, jax.numpy as jnp
        import numpy as np
        key = jax.random.key(seed)
        k1, k2 = jax.random.split(key)
        B, N, D = (4, 1024, 64)
        inp = jax.random.normal(k1, (B, N, D), dtype=jnp.float32)
        q_weight = jax.random.normal(k2, (D, D), dtype=jnp.float32)
        return {'input': inp, 'q_weight': q_weight}
    _L0_attn_all = _L0_attn_setup()
    _L0_attn_in = {k: v for k, v in _L0_attn_all.items() if k in ('q_weight',)}
    del _L0_attn_all

    def _L0_ffn_setup():
        import math
        import jax, jax.numpy as jnp
        import numpy as np
        CAPACITY_FACTOR = 1.25
        key = jax.random.key(seed)
        ks = jax.random.split(key, 5)
        B, L, D, F, E = (8, 2048, 64, 256, 8)
        h = jax.random.normal(ks[0], (B, L, D), dtype=jnp.float32)
        gate_w = jax.random.normal(ks[1], (D, E), dtype=jnp.float32) * 0.02
        gate_b = jnp.zeros((E,), dtype=jnp.float32)
        w1 = jax.random.normal(ks[2], (E, D, F), dtype=jnp.float32) * (1.0 / math.sqrt(D))
        b1 = jnp.zeros((E, F), dtype=jnp.float32)
        w2 = jax.random.normal(ks[3], (E, F, D), dtype=jnp.float32) * (1.0 / math.sqrt(F))
        b2 = jnp.zeros((E, D), dtype=jnp.float32)
        return {'h': h, 'gate_w': gate_w, 'gate_b': gate_b, 'w1': w1, 'b1': b1, 'w2': w2, 'b2': b2}
    _L0_ffn_all = _L0_ffn_setup()
    _L0_ffn_in = {k: v for k, v in _L0_ffn_all.items() if k in ('gate_w', 'gate_b', 'w1', 'b1', 'w2', 'b2')}
    del _L0_ffn_all

    def _L1_attn_setup():
        import jax, jax.numpy as jnp
        import numpy as np
        D_MODEL = 64
        N_HEAD = 8

        def _l1_scores(q, k):
            scale = 1.0 / np.sqrt(q.shape[-1]).astype(np.float32)
            q_sbhw = q.transpose(1, 0, 2, 3)

            def one_query(qs):
                return -jnp.sum(jnp.abs(qs[:, None, :, :] - k), axis=-1) * scale
            s = jax.lax.map(one_query, q_sbhw)
            return s.transpose(1, 0, 2, 3)
        key = jax.random.key(seed)
        ks = jax.random.split(key, 3)
        b, t = (4, 250)
        x = jax.random.normal(ks[0], (b, t, D_MODEL), jnp.float32)
        wqv_w = 0.005 * jax.random.normal(ks[1], (3 * N_HEAD * D_MODEL, D_MODEL), jnp.float32)
        wqv_b = jnp.zeros((3 * N_HEAD * D_MODEL,), jnp.float32)
        wk = 0.005 * jnp.ones((N_HEAD, D_MODEL), jnp.float32)
        fanin_w = 0.005 * jax.random.normal(ks[2], (D_MODEL, D_MODEL), jnp.float32)
        fanin_b = jnp.zeros((D_MODEL,), jnp.float32)
        return dict(x=x, wqv_w=wqv_w, wqv_b=wqv_b, wk=wk, fanin_w=fanin_w, fanin_b=fanin_b)
    _L1_attn_all = _L1_attn_setup()
    _L1_attn_in = {k: v for k, v in _L1_attn_all.items() if k in ('wqv_w', 'wqv_b', 'wk', 'fanin_w', 'fanin_b')}
    del _L1_attn_all

    def _L1_ffn_setup():
        import jax, jax.numpy as jnp
        import numpy as np
        NUM_EXPERTS = 8
        TOP_K = 2
        B, S, D = (8, 2048, 64)

        def _moe(tokens, router_w, w1, b1, w2, b2):
            N = tokens.shape[0]
            E = router_w.shape[0]
            logits = tokens.astype(jnp.float32) @ router_w.astype(jnp.float32).T
            probs = jax.nn.softmax(logits, axis=-1)
            rw, re = jax.lax.top_k(probs, TOP_K)
            if TOP_K > 1:
                rw = rw / jnp.maximum(rw.sum(-1, keepdims=True), 1e-12)
            rw = rw.astype(tokens.dtype)
            combine = jnp.zeros((N, E), tokens.dtype).at[jnp.arange(N)[:, None], re].set(rw)
            out = tokens
            for e in range(E):
                h = jax.nn.gelu(tokens @ w1[e] + b1[e], approximate=False)
                y = h @ w2[e] + b2[e]
                out = out + combine[:, e:e + 1] * y
            return out
        key = jax.random.key(seed)
        ks = jax.random.split(key, 4)
        scale = 1.0 / np.sqrt(D).astype(np.float32)
        return {'input_embeddings': jax.random.normal(ks[0], (B, S, D), jnp.float32), 'router_w': jax.random.normal(ks[1], (NUM_EXPERTS, D), jnp.float32) * scale, 'w1': jax.random.normal(ks[2], (NUM_EXPERTS, D, D), jnp.float32) * scale, 'b1': jnp.zeros((NUM_EXPERTS, D), jnp.float32), 'w2': jax.random.normal(ks[3], (NUM_EXPERTS, D, D), jnp.float32) * scale, 'b2': jnp.zeros((NUM_EXPERTS, D), jnp.float32)}
    _L1_ffn_all = _L1_ffn_setup()
    _L1_ffn_in = {k: v for k, v in _L1_ffn_all.items() if k in ('router_w', 'w1', 'b1', 'w2', 'b2')}
    del _L1_ffn_all

    def _L2_attn_setup():
        import jax, jax.numpy as jnp
        import numpy as np
        N, F, C, H = (32, 1024, 64, 8)
        D = C // H
        EPS_ATTN = 1e-06
        EPS_LN = 1e-05

        def layer_norm(x, g, b):
            mu = jnp.mean(x, axis=-1, keepdims=True)
            var = jnp.var(x, axis=-1, keepdims=True)
            return (x - mu) * jax.lax.rsqrt(var + EPS_LN) * g + b
        key = jax.random.key(seed)
        ks = jax.random.split(key, 8)
        s = 1.0 / np.sqrt(C)
        return {'x': jax.random.normal(ks[0], (N, F, C), jnp.float32), 'Wqkv': jax.random.uniform(ks[1], (3 * C, C), jnp.float32, -s, s), 'ln1_g': jnp.ones((C,), jnp.float32), 'ln1_b': jnp.zeros((C,), jnp.float32), 'W1': jax.random.uniform(ks[2], (C, C), jnp.float32, -s, s), 'b1': jax.random.uniform(ks[3], (C,), jnp.float32, -s, s), 'W2': jax.random.uniform(ks[4], (C, C), jnp.float32, -s, s), 'b2': jax.random.uniform(ks[5], (C,), jnp.float32, -s, s), 'ln2_g': jnp.ones((C,), jnp.float32), 'ln2_b': jnp.zeros((C,), jnp.float32)}
    _L2_attn_all = _L2_attn_setup()
    _L2_attn_in = {k: v for k, v in _L2_attn_all.items() if k in ('Wqkv', 'ln1_g', 'ln1_b', 'W1', 'b1', 'W2', 'b2', 'ln2_g', 'ln2_b')}
    del _L2_attn_all

    def _L2_ffn_setup():
        import math
        import jax, jax.numpy as jnp
        import numpy as np
        CAPACITY_FACTOR = 1.25
        TOP_K = 2
        LN_EPS = 1e-05

        def _layer_norm(x, gamma, beta):
            mu = jnp.mean(x, axis=-1, keepdims=True)
            var = jnp.var(x, axis=-1, keepdims=True)
            return (x - mu) * jax.lax.rsqrt(var + LN_EPS) * gamma + beta
        key = jax.random.key(seed)
        ks = jax.random.split(key, 4)
        B, S, D, F, E = (8, 1024, 64, 128, 8)
        x = jax.random.normal(ks[0], (B, S, D), dtype=jnp.float32)
        Wr = jax.random.normal(ks[1], (D, E), dtype=jnp.float32) / np.sqrt(D)
        br = jnp.zeros((E,), jnp.float32)
        W1 = jax.random.normal(ks[2], (E, D, F), dtype=jnp.float32) / np.sqrt(D)
        b1 = jnp.zeros((E, F), jnp.float32)
        W2 = jax.random.normal(ks[3], (E, F, D), dtype=jnp.float32) / np.sqrt(F)
        b2 = jnp.zeros((E, D), jnp.float32)
        gamma = jnp.ones((D,), jnp.float32)
        beta = jnp.zeros((D,), jnp.float32)
        return {'x': x, 'Wr': Wr, 'br': br, 'W1': W1, 'b1': b1, 'W2': W2, 'b2': b2, 'gamma': gamma, 'beta': beta}
    _L2_ffn_all = _L2_ffn_setup()
    _L2_ffn_in = {k: v for k, v in _L2_ffn_all.items() if k in ('Wr', 'br', 'W1', 'b1', 'W2', 'b2', 'gamma', 'beta')}
    del _L2_ffn_all

    def _L3_attn_setup():
        import jax, jax.numpy as jnp
        import numpy as np
        EPS_NORM = 1e-06
        EPS_ATTN = 1e-06
        HEADS = 8

        def rmsnorm(x, w):
            ms = jnp.mean(x * x, axis=-1, keepdims=True)
            return w * (x * jax.lax.rsqrt(ms + EPS_NORM))

        def linear_attention(x, w_qkv, w_out, b_out):
            B, N, D = x.shape
            hd = D // HEADS
            qkv = (x @ w_qkv).reshape(B, N, 3, HEADS, hd)
            q, k, v = (qkv[:, :, 0], qkv[:, :, 1], qkv[:, :, 2])
            q = jax.nn.elu(q) + 1.0
            k = jax.nn.elu(k) + 1.0
            kv = jnp.einsum('bnhd,bnhm->bhdm', k, v)
            z = 1.0 / (jnp.einsum('bnhd,bhd->bnh', q, k.sum(axis=1)) + EPS_ATTN)
            out = jnp.einsum('bnhd,bhdm,bnh->bnhm', q, kv, z)
            out = out.reshape(B, N, D)
            return out @ w_out + b_out
        key = jax.random.key(seed)
        ks = jax.random.split(key, 4)
        B, N, D = (16, 2048, 64)
        x = jax.random.normal(ks[0], (B, N, D), dtype=jnp.float32)
        w_norm1 = jnp.ones((D,), dtype=jnp.float32)
        w_qkv = jax.random.normal(ks[1], (D, 3 * D), dtype=jnp.float32) * 0.02
        w_out = jax.random.normal(ks[2], (D, D), dtype=jnp.float32) * 0.02
        b_out = jnp.zeros((D,), dtype=jnp.float32)
        w_norm2 = jnp.ones((D,), dtype=jnp.float32)
        return {'x': x, 'w_norm1': w_norm1, 'w_qkv': w_qkv, 'w_out': w_out, 'b_out': b_out, 'w_norm2': w_norm2}
    _L3_attn_all = _L3_attn_setup()
    _L3_attn_in = {k: v for k, v in _L3_attn_all.items() if k in ('w_norm1', 'w_qkv', 'w_out', 'b_out', 'w_norm2')}
    del _L3_attn_all

    def _L3_ffn_setup():
        import jax, jax.numpy as jnp
        import numpy as np
        B, N, D = (16, 1024, 64)
        NUM_EXPERTS, TOP_K, HEADS = (4, 2, 4)
        N_EDGES = 262144
        LN_EPS = 1e-05

        def _layernorm(x, g, b):
            mu = x.mean(-1, keepdims=True)
            var = ((x - mu) ** 2).mean(-1, keepdims=True)
            return (x - mu) * jax.lax.rsqrt(var + LN_EPS) * g + b

        def _forward(x, edge_index, W_gat, att_src, att_dst, b_gat, ln_gamma, ln_beta, W1, b1, W2, b2):
            Bc, Nc, Dc = x.shape
            M = Bc * Nc
            x_flat = x.reshape(M, Dc)
            h = (x_flat @ W_gat).reshape(M, HEADS, NUM_EXPERTS)
            loops = jnp.arange(M, dtype=edge_index.dtype)
            src = jnp.concatenate([edge_index[0], loops])
            dst = jnp.concatenate([edge_index[1], loops])
            a_src = (h * att_src).sum(-1)
            a_dst = (h * att_dst).sum(-1)
            e = jax.nn.leaky_relu(a_src[src] + a_dst[dst], negative_slope=0.2)
            e_max = jax.ops.segment_max(e, dst, num_segments=M)
            ee = jnp.exp(e - e_max[dst])
            denom = jax.ops.segment_sum(ee, dst, num_segments=M)
            alpha = ee / (denom[dst] + 1e-16)
            msg = h[src] * alpha[:, :, None]
            agg = jax.ops.segment_sum(msg, dst, num_segments=M).reshape(M, HEADS * NUM_EXPERTS) + b_gat
            scores = _layernorm(agg, ln_gamma, ln_beta).reshape(M, HEADS, NUM_EXPERTS).mean(1)
            scores = scores.reshape(Bc, Nc, NUM_EXPERTS)
            topk_s, topk_i = jax.lax.top_k(scores, TOP_K)
            w = jax.nn.softmax(topk_s, axis=-1)
            out = jnp.zeros_like(x)
            for ei in range(NUM_EXPERTS):
                g = jnp.where(topk_i == ei, w, 0.0).sum(-1)
                hh = jax.nn.gelu(x @ W1[ei] + b1[ei], approximate=False)
                out = out + g[..., None] * (hh @ W2[ei] + b2[ei])
            return out
        key = jax.random.key(seed)
        ks = jax.random.split(key, 8)
        s = 0.05
        return {'x': jax.random.normal(ks[0], (B, N, D), jnp.float32), 'W_gat': jax.random.normal(ks[1], (D, HEADS * NUM_EXPERTS), jnp.float32) * s, 'att_src': jax.random.normal(ks[2], (HEADS, NUM_EXPERTS), jnp.float32) * s, 'att_dst': jax.random.normal(ks[3], (HEADS, NUM_EXPERTS), jnp.float32) * s, 'b_gat': jnp.zeros((HEADS * NUM_EXPERTS,), jnp.float32), 'ln_gamma': jnp.ones((HEADS * NUM_EXPERTS,), jnp.float32), 'ln_beta': jnp.zeros((HEADS * NUM_EXPERTS,), jnp.float32), 'W1': jax.random.normal(ks[4], (NUM_EXPERTS, D, 2 * D), jnp.float32) * s, 'b1': jnp.zeros((NUM_EXPERTS, 2 * D), jnp.float32), 'W2': jax.random.normal(ks[5], (NUM_EXPERTS, 2 * D, D), jnp.float32) * s, 'b2': jnp.zeros((NUM_EXPERTS, D), jnp.float32), 'edge_index': jax.random.randint(ks[6], (2, N_EDGES), 0, B * N, jnp.int32)}
    _L3_ffn_all = _L3_ffn_setup()
    _L3_ffn_in = {k: v for k, v in _L3_ffn_all.items() if k in ('W_gat', 'att_src', 'att_dst', 'b_gat', 'ln_gamma', 'ln_beta', 'W1', 'b1', 'W2', 'b2', 'edge_index')}
    del _L3_ffn_all
    return {'x': x, 'L0_tok_p_w': _L0_tok_in['p_w'], 'L0_tok_p_b': _L0_tok_in['p_b'], 'L0_tok_fw': _L0_tok_in['fw'], 'L0_tok_w1_w': _L0_tok_in['w1_w'], 'L0_tok_w1_b': _L0_tok_in['w1_b'], 'L0_tok_w2_w': _L0_tok_in['w2_w'], 'L0_tok_w2_b': _L0_tok_in['w2_b'], 'L0_tok_q1_w': _L0_tok_in['q1_w'], 'L0_tok_q1_b': _L0_tok_in['q1_b'], 'L0_tok_q2_w': _L0_tok_in['q2_w'], 'L0_tok_q2_b': _L0_tok_in['q2_b'], 'L0_attn_q_weight': _L0_attn_in['q_weight'], 'L0_ffn_gate_w': _L0_ffn_in['gate_w'], 'L0_ffn_gate_b': _L0_ffn_in['gate_b'], 'L0_ffn_w1': _L0_ffn_in['w1'], 'L0_ffn_b1': _L0_ffn_in['b1'], 'L0_ffn_w2': _L0_ffn_in['w2'], 'L0_ffn_b2': _L0_ffn_in['b2'], 'L1_attn_wqv_w': _L1_attn_in['wqv_w'], 'L1_attn_wqv_b': _L1_attn_in['wqv_b'], 'L1_attn_wk': _L1_attn_in['wk'], 'L1_attn_fanin_w': _L1_attn_in['fanin_w'], 'L1_attn_fanin_b': _L1_attn_in['fanin_b'], 'L1_ffn_router_w': _L1_ffn_in['router_w'], 'L1_ffn_w1': _L1_ffn_in['w1'], 'L1_ffn_b1': _L1_ffn_in['b1'], 'L1_ffn_w2': _L1_ffn_in['w2'], 'L1_ffn_b2': _L1_ffn_in['b2'], 'L2_attn_Wqkv': _L2_attn_in['Wqkv'], 'L2_attn_ln1_g': _L2_attn_in['ln1_g'], 'L2_attn_ln1_b': _L2_attn_in['ln1_b'], 'L2_attn_W1': _L2_attn_in['W1'], 'L2_attn_b1': _L2_attn_in['b1'], 'L2_attn_W2': _L2_attn_in['W2'], 'L2_attn_b2': _L2_attn_in['b2'], 'L2_attn_ln2_g': _L2_attn_in['ln2_g'], 'L2_attn_ln2_b': _L2_attn_in['ln2_b'], 'L2_ffn_Wr': _L2_ffn_in['Wr'], 'L2_ffn_br': _L2_ffn_in['br'], 'L2_ffn_W1': _L2_ffn_in['W1'], 'L2_ffn_b1': _L2_ffn_in['b1'], 'L2_ffn_W2': _L2_ffn_in['W2'], 'L2_ffn_b2': _L2_ffn_in['b2'], 'L2_ffn_gamma': _L2_ffn_in['gamma'], 'L2_ffn_beta': _L2_ffn_in['beta'], 'L3_attn_w_norm1': _L3_attn_in['w_norm1'], 'L3_attn_w_qkv': _L3_attn_in['w_qkv'], 'L3_attn_w_out': _L3_attn_in['w_out'], 'L3_attn_b_out': _L3_attn_in['b_out'], 'L3_attn_w_norm2': _L3_attn_in['w_norm2'], 'L3_ffn_W_gat': _L3_ffn_in['W_gat'], 'L3_ffn_att_src': _L3_ffn_in['att_src'], 'L3_ffn_att_dst': _L3_ffn_in['att_dst'], 'L3_ffn_b_gat': _L3_ffn_in['b_gat'], 'L3_ffn_ln_gamma': _L3_ffn_in['ln_gamma'], 'L3_ffn_ln_beta': _L3_ffn_in['ln_beta'], 'L3_ffn_W1': _L3_ffn_in['W1'], 'L3_ffn_b1': _L3_ffn_in['b1'], 'L3_ffn_W2': _L3_ffn_in['W2'], 'L3_ffn_b2': _L3_ffn_in['b2'], 'L3_ffn_edge_index': _L3_ffn_in['edge_index']}

def reference(x, L0_tok_p_w, L0_tok_p_b, L0_tok_fw, L0_tok_w1_w, L0_tok_w1_b, L0_tok_w2_w, L0_tok_w2_b, L0_tok_q1_w, L0_tok_q1_b, L0_tok_q2_w, L0_tok_q2_b, L0_attn_q_weight, L0_ffn_gate_w, L0_ffn_gate_b, L0_ffn_w1, L0_ffn_b1, L0_ffn_w2, L0_ffn_b2, L1_attn_wqv_w, L1_attn_wqv_b, L1_attn_wk, L1_attn_fanin_w, L1_attn_fanin_b, L1_ffn_router_w, L1_ffn_w1, L1_ffn_b1, L1_ffn_w2, L1_ffn_b2, L2_attn_Wqkv, L2_attn_ln1_g, L2_attn_ln1_b, L2_attn_W1, L2_attn_b1, L2_attn_W2, L2_attn_b2, L2_attn_ln2_g, L2_attn_ln2_b, L2_ffn_Wr, L2_ffn_br, L2_ffn_W1, L2_ffn_b1, L2_ffn_W2, L2_ffn_b2, L2_ffn_gamma, L2_ffn_beta, L3_attn_w_norm1, L3_attn_w_qkv, L3_attn_w_out, L3_attn_b_out, L3_attn_w_norm2, L3_ffn_W_gat, L3_ffn_att_src, L3_ffn_att_dst, L3_ffn_b_gat, L3_ffn_ln_gamma, L3_ffn_ln_beta, L3_ffn_W1, L3_ffn_b1, L3_ffn_W2, L3_ffn_b2, L3_ffn_edge_index):
    import jax
    import jax.numpy as jnp

    def _L0_tok_ref(x, p_w, p_b, fw, w1_w, w1_b, w2_w, w2_b, q1_w, q1_b, q2_w, q2_b):
        import jax, jax.numpy as jnp
        import numpy as np
        B, S, D_A, D_V, D_U, L, M1, M2 = (16, 64, 3, 32, 1, 4, 12, 12)
        MID = 4 * D_U

        def conv1x1(x, w, b):
            return jnp.einsum('bixy,oi->boxy', x, w) + b[None, :, None, None]

        def fourier_layer(x, fw_i):
            Bm, C, M, N = x.shape
            x_ft = jnp.fft.rfft2(x, s=(M, N), norm='ortho')
            w_lo = fw_i[0, ..., 0] + 1j * fw_i[0, ..., 1]
            w_hi = fw_i[1, ..., 0] + 1j * fw_i[1, ..., 1]
            lo = jnp.einsum('bixy,ioxy->boxy', x_ft[:, :, :M1, :M2], w_lo)
            hi = jnp.einsum('bixy,ioxy->boxy', x_ft[:, :, -M1:, :M2], w_hi)
            out_ft = jnp.zeros(x_ft.shape, dtype=x_ft.dtype)
            out_ft = out_ft.at[:, :, :M1, :M2].set(lo)
            out_ft = out_ft.at[:, :, -M1:, :M2].set(hi)
            return jnp.fft.irfft2(out_ft, s=(M, N), norm='ortho')

        def make_grid(b, sx, sy):
            gx = jnp.broadcast_to(jnp.linspace(0.0, 1.0, sx)[None, :, None], (b, sx, sy))
            gy = jnp.broadcast_to(jnp.linspace(0.0, 1.0, sy)[None, None, :], (b, sx, sy))
            return jnp.stack([gx, gy], axis=-1)
        b, sx, sy = (x.shape[0], x.shape[1], x.shape[2])
        grid = make_grid(b, sx, sy)
        h = jnp.concatenate([x, grid], axis=-1)
        h = jnp.transpose(h, (0, 3, 1, 2))
        h = conv1x1(h, p_w, p_b)
        for i in range(L):
            x1 = fourier_layer(h, fw[i])
            x1 = jax.nn.relu(conv1x1(x1, w1_w[i], w1_b[i]))
            x1 = conv1x1(x1, w2_w[i], w2_b[i])
            h = h + x1
        h = conv1x1(h, q1_w, q1_b)
        h = jax.nn.relu(h)
        h = conv1x1(h, q2_w, q2_b)
        return jnp.squeeze(h)

    def _L0_attn_ref(input, q_weight):
        import jax, jax.numpy as jnp
        import numpy as np
        query = jnp.einsum('bnd,de->bne', input, q_weight)
        att = jax.nn.sigmoid(jnp.einsum('bnd,bmd->bnm', query, input))
        value = jnp.einsum('bnm,bmd->bnd', att, input)
        return value

    def _L0_ffn_ref(h, gate_w, gate_b, w1, b1, w2, b2):
        import math
        import jax, jax.numpy as jnp
        import numpy as np
        CAPACITY_FACTOR = 1.25
        B, L, D = h.shape
        E = gate_w.shape[1]
        T = B * L
        C = max(1, math.ceil(CAPACITY_FACTOR * T / E))
        x = h.reshape(T, D)
        logits = x @ gate_w + gate_b
        probs = jax.nn.softmax(logits, axis=-1)
        idx = jnp.argmax(probs, axis=-1)
        prb = jnp.take_along_axis(probs, idx[:, None], axis=1)[:, 0]
        one_hot = jax.nn.one_hot(idx, E, dtype=jnp.float32)
        pos = (jnp.cumsum(one_hot, axis=0) * one_hot).sum(-1).astype(jnp.int32) - 1
        kept = pos < C
        pos_safe = jnp.where(kept, pos, C)
        buf = jnp.zeros((E, C, D), dtype=h.dtype).at[idx, pos_safe].set(x, mode='drop')
        hmid = jax.nn.relu(jnp.einsum('ecd,edf->ecf', buf, w1) + b1[:, None, :])
        ybuf = jnp.einsum('ecf,efd->ecd', hmid, w2) + b2[:, None, :]
        pos_g = jnp.minimum(pos, C - 1)
        y_tok = ybuf[idx, pos_g] * (prb * kept)[:, None]
        y = y_tok.reshape(B, L, D)
        y = jnp.nan_to_num(y, nan=0.0, posinf=10000.0, neginf=-10000.0)
        return y

    def _L1_attn_ref(x, wqv_w, wqv_b, wk, fanin_w, fanin_b):
        import jax, jax.numpy as jnp
        import numpy as np
        D_MODEL = 64
        N_HEAD = 8

        def _l1_scores(q, k):
            scale = 1.0 / np.sqrt(q.shape[-1]).astype(np.float32)
            q_sbhw = q.transpose(1, 0, 2, 3)

            def one_query(qs):
                return -jnp.sum(jnp.abs(qs[:, None, :, :] - k), axis=-1) * scale
            s = jax.lax.map(one_query, q_sbhw)
            return s.transpose(1, 0, 2, 3)
        b, t, d = x.shape
        h = N_HEAD
        v = (x @ wqv_w.T + wqv_b).reshape(b, t, 3 * h, d)
        q, vf, vb = (v[:, :, :h], v[:, :, h:2 * h], v[:, :, 2 * h:])
        k = x[:, :, None, :] * wk[None, None]
        a = _l1_scores(q, k)
        a = jnp.concatenate([a, jnp.zeros((b, 1, t, h), a.dtype)], axis=1)
        a = jax.nn.softmax(a, axis=1)[:, :t]
        bf = jnp.einsum('bsdh,bshw->bdhw', a, vf)
        bb = jnp.einsum('bdsh,bshw->bdhw', a, vb)
        o = (bf + bb).sum(axis=2).reshape(b, t, d)
        y = o * jax.nn.sigmoid(1.702 * o)
        y = y @ fanin_w.T + fanin_b
        return x + y

    def _L1_ffn_ref(input_embeddings, router_w, w1, b1, w2, b2):
        import jax, jax.numpy as jnp
        import numpy as np
        NUM_EXPERTS = 8
        TOP_K = 2
        B, S, D = (8, 2048, 64)

        def _moe(tokens, router_w, w1, b1, w2, b2):
            N = tokens.shape[0]
            E = router_w.shape[0]
            logits = tokens.astype(jnp.float32) @ router_w.astype(jnp.float32).T
            probs = jax.nn.softmax(logits, axis=-1)
            rw, re = jax.lax.top_k(probs, TOP_K)
            if TOP_K > 1:
                rw = rw / jnp.maximum(rw.sum(-1, keepdims=True), 1e-12)
            rw = rw.astype(tokens.dtype)
            combine = jnp.zeros((N, E), tokens.dtype).at[jnp.arange(N)[:, None], re].set(rw)
            out = tokens
            for e in range(E):
                h = jax.nn.gelu(tokens @ w1[e] + b1[e], approximate=False)
                y = h @ w2[e] + b2[e]
                out = out + combine[:, e:e + 1] * y
            return out
        b, s, d = input_embeddings.shape
        tokens = input_embeddings.reshape(b * s, d)
        return _moe(tokens, router_w, w1, b1, w2, b2).reshape(b, s, d)

    def _L2_attn_ref(x, Wqkv, ln1_g, ln1_b, W1, b1, W2, b2, ln2_g, ln2_b):
        import jax, jax.numpy as jnp
        import numpy as np
        N, F, C, H = (32, 1024, 64, 8)
        D = C // H
        EPS_ATTN = 1e-06
        EPS_LN = 1e-05

        def layer_norm(x, g, b):
            mu = jnp.mean(x, axis=-1, keepdims=True)
            var = jnp.var(x, axis=-1, keepdims=True)
            return (x - mu) * jax.lax.rsqrt(var + EPS_LN) * g + b
        n, f, c = x.shape
        qkv = jnp.einsum('nfc,oc->nfo', x, Wqkv)
        q, k, v = jnp.split(qkv, 3, axis=-1)
        q = q.reshape(n, f, H, D)
        k = k.reshape(n, f, H, D)
        v = v.reshape(n, f, H, D)
        q = jax.nn.elu(q) + 1.0
        k = jax.nn.elu(k) + 1.0
        kv = jnp.einsum('nshd,nshm->nhmd', k, v)
        ksum = jnp.sum(k, axis=1)
        z = 1.0 / (jnp.einsum('nlhd,nhd->nlh', q, ksum) + EPS_ATTN)
        t = jnp.einsum('nlhd,nhmd,nlh->nlhm', q, kv, z)
        t = t.reshape(n, f, c)
        x1 = layer_norm(t + x, ln1_g, ln1_b)
        h = jax.nn.gelu(jnp.einsum('nfc,oc->nfo', x1, W1) + b1, approximate=False)
        y = jnp.einsum('nfc,oc->nfo', h, W2) + b2
        return layer_norm(y + x1, ln2_g, ln2_b)

    def _L2_ffn_ref(x, Wr, br, W1, b1, W2, b2, gamma, beta):
        import math
        import jax, jax.numpy as jnp
        import numpy as np
        CAPACITY_FACTOR = 1.25
        TOP_K = 2
        LN_EPS = 1e-05

        def _layer_norm(x, gamma, beta):
            mu = jnp.mean(x, axis=-1, keepdims=True)
            var = jnp.var(x, axis=-1, keepdims=True)
            return (x - mu) * jax.lax.rsqrt(var + LN_EPS) * gamma + beta
        B, S, D = x.shape
        E = Wr.shape[1]
        N = B * S
        K = TOP_K
        logits = jnp.mean(x, axis=1) @ Wr + br
        routing_weights = jax.nn.softmax(logits, axis=-1)
        capacity = float(math.ceil(N * CAPACITY_FACTOR / E))
        expected_loads = routing_weights.sum(axis=0) * (N / B)
        scale = jnp.where(expected_loads > capacity, capacity / expected_loads, 1.0)
        routing_weights = jax.nn.softmax(routing_weights * scale, axis=-1)
        rw_tok = jnp.broadcast_to(routing_weights[:, None, :], (B, S, E)).reshape(N, E)
        top_w, top_i = jax.lax.top_k(rw_tok, K)
        top_w = jax.nn.softmax(top_w, axis=-1)
        xf = x.reshape(N, D)
        h = jax.nn.gelu(jnp.einsum('nd,edf->enf', xf, W1) + b1[:, None, :], approximate=False)
        y = jnp.einsum('enf,efd->end', h, W2) + b2[:, None, :]
        w_dense = jnp.zeros((N, E), x.dtype).at[jnp.arange(N)[:, None], top_i].add(top_w)
        out = jnp.einsum('ne,end->nd', w_dense, y).reshape(B, S, D)
        out = _layer_norm(out + x, gamma, beta)
        return out

    def _L3_attn_ref(x, w_norm1, w_qkv, w_out, b_out, w_norm2):
        import jax, jax.numpy as jnp
        import numpy as np
        EPS_NORM = 1e-06
        EPS_ATTN = 1e-06
        HEADS = 8

        def rmsnorm(x, w):
            ms = jnp.mean(x * x, axis=-1, keepdims=True)
            return w * (x * jax.lax.rsqrt(ms + EPS_NORM))

        def linear_attention(x, w_qkv, w_out, b_out):
            B, N, D = x.shape
            hd = D // HEADS
            qkv = (x @ w_qkv).reshape(B, N, 3, HEADS, hd)
            q, k, v = (qkv[:, :, 0], qkv[:, :, 1], qkv[:, :, 2])
            q = jax.nn.elu(q) + 1.0
            k = jax.nn.elu(k) + 1.0
            kv = jnp.einsum('bnhd,bnhm->bhdm', k, v)
            z = 1.0 / (jnp.einsum('bnhd,bhd->bnh', q, k.sum(axis=1)) + EPS_ATTN)
            out = jnp.einsum('bnhd,bhdm,bnh->bnhm', q, kv, z)
            out = out.reshape(B, N, D)
            return out @ w_out + b_out
        h = x + linear_attention(rmsnorm(x, w_norm1), w_qkv, w_out, b_out)
        return h + rmsnorm(h, w_norm2)

    def _L3_ffn_ref(x, W_gat, att_src, att_dst, b_gat, ln_gamma, ln_beta, W1, b1, W2, b2, edge_index):
        import jax, jax.numpy as jnp
        import numpy as np
        B, N, D = (16, 1024, 64)
        NUM_EXPERTS, TOP_K, HEADS = (4, 2, 4)
        N_EDGES = 262144
        LN_EPS = 1e-05

        def _layernorm(x, g, b):
            mu = x.mean(-1, keepdims=True)
            var = ((x - mu) ** 2).mean(-1, keepdims=True)
            return (x - mu) * jax.lax.rsqrt(var + LN_EPS) * g + b

        def _forward(x, edge_index, W_gat, att_src, att_dst, b_gat, ln_gamma, ln_beta, W1, b1, W2, b2):
            Bc, Nc, Dc = x.shape
            M = Bc * Nc
            x_flat = x.reshape(M, Dc)
            h = (x_flat @ W_gat).reshape(M, HEADS, NUM_EXPERTS)
            loops = jnp.arange(M, dtype=edge_index.dtype)
            src = jnp.concatenate([edge_index[0], loops])
            dst = jnp.concatenate([edge_index[1], loops])
            a_src = (h * att_src).sum(-1)
            a_dst = (h * att_dst).sum(-1)
            e = jax.nn.leaky_relu(a_src[src] + a_dst[dst], negative_slope=0.2)
            e_max = jax.ops.segment_max(e, dst, num_segments=M)
            ee = jnp.exp(e - e_max[dst])
            denom = jax.ops.segment_sum(ee, dst, num_segments=M)
            alpha = ee / (denom[dst] + 1e-16)
            msg = h[src] * alpha[:, :, None]
            agg = jax.ops.segment_sum(msg, dst, num_segments=M).reshape(M, HEADS * NUM_EXPERTS) + b_gat
            scores = _layernorm(agg, ln_gamma, ln_beta).reshape(M, HEADS, NUM_EXPERTS).mean(1)
            scores = scores.reshape(Bc, Nc, NUM_EXPERTS)
            topk_s, topk_i = jax.lax.top_k(scores, TOP_K)
            w = jax.nn.softmax(topk_s, axis=-1)
            out = jnp.zeros_like(x)
            for ei in range(NUM_EXPERTS):
                g = jnp.where(topk_i == ei, w, 0.0).sum(-1)
                hh = jax.nn.gelu(x @ W1[ei] + b1[ei], approximate=False)
                out = out + g[..., None] * (hh @ W2[ei] + b2[ei])
            return out
        return _forward(x, edge_index, W_gat, att_src, att_dst, b_gat, ln_gamma, ln_beta, W1, b1, W2, b2)
    h = _L0_tok_ref(x, L0_tok_p_w, L0_tok_p_b, L0_tok_fw, L0_tok_w1_w, L0_tok_w1_b, L0_tok_w2_w, L0_tok_w2_b, L0_tok_q1_w, L0_tok_q1_b, L0_tok_q2_w, L0_tok_q2_b)
    h = h + _L0_attn_ref(_layernorm(h, axis=-1), L0_attn_q_weight)
    h = h + _L0_ffn_ref(_layernorm(h, axis=-1), L0_ffn_gate_w, L0_ffn_gate_b, L0_ffn_w1, L0_ffn_b1, L0_ffn_w2, L0_ffn_b2)
    h = h + _L1_attn_ref(_layernorm(h, axis=-1), L1_attn_wqv_w, L1_attn_wqv_b, L1_attn_wk, L1_attn_fanin_w, L1_attn_fanin_b)
    h = h + _L1_ffn_ref(_layernorm(h, axis=-1), L1_ffn_router_w, L1_ffn_w1, L1_ffn_b1, L1_ffn_w2, L1_ffn_b2)
    h = h + _L2_attn_ref(_layernorm(h, axis=-1), L2_attn_Wqkv, L2_attn_ln1_g, L2_attn_ln1_b, L2_attn_W1, L2_attn_b1, L2_attn_W2, L2_attn_b2, L2_attn_ln2_g, L2_attn_ln2_b)
    h = h + _L2_ffn_ref(_layernorm(h, axis=-1), L2_ffn_Wr, L2_ffn_br, L2_ffn_W1, L2_ffn_b1, L2_ffn_W2, L2_ffn_b2, L2_ffn_gamma, L2_ffn_beta)
    h = h + _L3_attn_ref(_layernorm(h, axis=-1), L3_attn_w_norm1, L3_attn_w_qkv, L3_attn_w_out, L3_attn_b_out, L3_attn_w_norm2)
    h = h + _L3_ffn_ref(_layernorm(h, axis=-1), L3_ffn_W_gat, L3_ffn_att_src, L3_ffn_att_dst, L3_ffn_b_gat, L3_ffn_ln_gamma, L3_ffn_ln_beta, L3_ffn_W1, L3_ffn_b1, L3_ffn_W2, L3_ffn_b2, L3_ffn_edge_index)
    return h

_drawn_inputs = setup_inputs


def setup_inputs(seed=0):
    import zlib

    import numpy as np

    out = dict(_drawn_inputs(seed))
    spreads = {'L0_tok_p_b': (0.0, 0.1),
     'L0_tok_w1_b': (0.0, 0.1),
     'L0_tok_w2_b': (0.0, 0.1),
     'L0_tok_q1_b': (0.0, 0.1),
     'L0_ffn_gate_b': (0.0, 0.8),
     'L0_ffn_b1': (0.0, 0.8),
     'L0_ffn_b2': (0.0, 2.0),
     'L1_attn_wqv_b': (0.0, 0.8),
     'L1_attn_wk': (0.004999999888241291, 0.6),
     'L1_attn_fanin_b': (0.0, 0.8),
     'L1_ffn_b1': (0.0, 0.8),
     'L1_ffn_b2': (0.0, 0.8),
     'L2_attn_ln1_g': (1.0, 0.6),
     'L2_attn_ln1_b': (0.0, 0.8),
     'L2_attn_ln2_g': (1.0, 0.6),
     'L2_attn_ln2_b': (0.0, 0.8),
     'L2_ffn_br': (0.0, 0.612),
     'L2_ffn_b1': (0.0, 0.8),
     'L2_ffn_b2': (0.0, 0.8),
     'L2_ffn_gamma': (1.0, 0.6),
     'L2_ffn_beta': (0.0, 0.8),
     'L3_attn_w_norm1': (1.0, 0.6),
     'L3_attn_b_out': (0.0, 0.682),
     'L3_attn_w_norm2': (1.0, 0.6),
     'L3_ffn_b_gat': (0.0, 0.8),
     'L3_ffn_ln_gamma': (1.0, 0.6),
     'L3_ffn_ln_beta': (0.0, 0.8),
     'L3_ffn_b1': (0.0, 0.8),
     'L3_ffn_b2': (0.0, 2.0)}
    factors = {'L0_ffn_gate_w': 8.0,
     'L0_ffn_w1': 8.0,
     'L0_ffn_w2': 8.0,
     'L1_attn_wqv_w': 21.679,
     'L1_attn_fanin_w': 8.0,
     'L2_attn_W1': 4.109,
     'L2_attn_b1': 8.0,
     'L2_attn_W2': 3.872,
     'L2_attn_b2': 8.0,
     'L3_attn_w_qkv': 8.0,
     'L3_attn_w_out': 8.0,
     'L3_ffn_W_gat': 8.0,
     'L3_ffn_att_src': 8.0,
     'L3_ffn_att_dst': 8.0,
     'L3_ffn_W1': 8.0,
     'L3_ffn_W2': 8.0}
    for name, (base, spread) in spreads.items():
        noise = np.random.default_rng([zlib.crc32(name.encode()), seed]).standard_normal(out[name].shape)
        drawn = base * np.exp(spread * noise) if base else spread * noise
        out[name] = jnp.asarray(drawn.astype(out[name].dtype))
    for name, factor in factors.items():
        out[name] = (out[name] * factor).astype(out[name].dtype)
    return out
```

```python
import numpy as np
from contextlib import ExitStack, contextmanager
import concourse.bass as bass
from concourse import mybir

F32 = mybir.dt.float32
I32 = mybir.dt.int32
BF16 = mybir.dt.bfloat16
ALU = mybir.AluOpType
ACT = mybir.ActivationFunctionType
AX = mybir.AxisListType.X

P = 128
NB = 128
S = 64
D = 64
TILES = NB * S // P
IT = 16
STEPS = TILES // IT
GT = 4
G = IT // GT


class Tower:

    def __init__(self, nc, ctx):
        self.nc = nc
        self.ctx = ctx
        self.bank = [ctx.enter_context(nc.psum_tensor(f"bank{i}", [P, 512], F32)) for i in range(8)]
        self.sems = {}
        self.const = {}
        self.built = {}

    def name_constants(self):
        c = self.const
        self.ident, self.ones, self.upto, self.before, self.iota = c["ident"], c["ones"], c["upto"], c["before"], c["iota"]
        self.falling, self.heads, self.halves, self.own_tile, self.own_half = c["falling"], c["heads"], c["halves"], c["own_tile"], c["own_half"]
        self.of_image, self.same_image, self.pick_row = c["of_image"], c["same_image"], c["pick_row"]

    def sb(self, name, shape, dt=F32, ctx=None):
        n = self.built[name] = self.built.get(name, 0) + 1
        return (ctx or self.ctx).enter_context(self.nc.sbuf_tensor(name if n == 1 else f"{name}_{n}", list(shape), dt))

    def sem(self, name):
        if name not in self.sems:
            self.sems[name] = self.ctx.enter_context(self.nc.semaphore(name))
        return self.sems[name]

    @contextmanager
    def stage(self, *names):
        nc = self.nc
        sems = [self.sem(n) for n in names]
        with nc.Block() as block:
            yield (block, *sems)
        nc.all_engine_barrier()
        for n, s in zip(names, sems):
            if n.startswith("pool_"):
                nc.gpsimd.dma_reset(range(s.num, s.num + 1))
            nc.gpsimd.sem_clear(s)
        nc.all_engine_barrier()


class Chain:

    def __init__(self, eng, sem):
        self.eng, self.sem, self.n = eng, sem, 0

    def link(self, ins):
        self.n += 1
        ins.then_inc(self.sem, 1)
        self.eng.wait_ge(self.sem, self.n)


def bc(ap, n):
    return ap.unsqueeze(2).broadcast_to([ap.shape[0], ap.shape[1], n])


LAYERS, CH, M1, M2 = 4, 32, 12, 12
KX, KYG, KQ = 2 * M1, 3, 4
GI = 32
IGROUPS = NB // GI
PAIRS = GI // 2
CHUNK = 8
CHUNKS = GI // CHUNK
CC = CH // 8


def fno_constants():
    n = np.arange(S)
    kx = np.concatenate([np.arange(M1), np.arange(-M1, 0)])
    ax = 2 * np.pi * np.outer(kx, n) / S
    c = {}
    s1 = np.zeros((KX, 2, 2, 2, S))
    for g in range(2):
        s1[:, 0, g, g] = np.cos(ax) / 8
        s1[:, 1, g, g] = -np.sin(ax) / 8
    c["to_x"] = s1.reshape(KX * 4, 2 * S)
    s2 = np.zeros((4, KQ, KYG, 2, 2, 4, 32))
    f1 = np.zeros((4, 32, 2, 2, KYG, KQ, 4))
    fx = np.zeros((S, 2, KYG, KQ))
    for kq in range(KQ):
        for kg in range(KYG):
            ky = 4 * kg + kq
            w = (1 if ky == 0 else 2) / 8
            ay = 2 * np.pi * ky * n / S
            for cc in range(4):
                s2[cc, kq, kg, 0, :, cc] = (w * np.cos(ay)).reshape(2, 32)
                s2[cc, kq, kg, 1, :, cc] = (-w * np.sin(ay)).reshape(2, 32)
                f1[cc, :, :, 0, kg, kq, cc] = (np.cos(ay) / 8).reshape(2, 32).T
                f1[cc, :, :, 1, kg, kq, cc] = (-np.sin(ay) / 8).reshape(2, 32).T
            fx[:, 0, kg, kq] = np.cos(ay) / 8
            fx[:, 1, kg, kq] = -np.sin(ay) / 8
    c["to_y"] = s2.reshape(96, 2 * P)
    c["from_y"] = f1.reshape(P, 2 * 96)
    c["from_y1"] = fx.reshape(S, 24)
    f2 = np.zeros((2, S, 2, KX, 2, 2))
    for m in range(2):
        f2[m, :, 0, :, 0, m] = np.cos(ax).T / 8
        f2[m, :, 0, :, 1, m] = -np.sin(ax).T / 8
        f2[m, :, 1, :, 0, m] = np.sin(ax).T / 8
        f2[m, :, 1, :, 1, m] = np.cos(ax).T / 8
    c["from_x"] = f2.reshape(P, 2 * 96)
    lin = np.linspace(0.0, 1.0, S, dtype=np.float32).astype(np.float64)
    feats = [np.repeat(lin[:, None], S, 1), np.repeat(lin[None], S, 0), np.ones((S, S))]
    sp = np.zeros((4, KQ, KYG, KX, 2, GI))
    for f, v in enumerate(feats):
        ft = np.fft.rfft2(v, norm="ortho")
        for kq in range(KQ):
            for kg in range(KYG):
                col = ft[kx, 4 * kg + kq]
                sp[f + 1, kq, kg, :, 0] = col.real[:, None]
                sp[f + 1, kq, kg, :, 1] = col.imag[:, None]
    c["grid_spectrum"] = sp.reshape(16, KYG * KX * 2 * GI)
    c["eye32"] = np.tile(np.eye(32), (4, 1))
    return {k: np.ascontiguousarray(v.astype(np.float32)) for k, v in c.items()}


def channel(cg, cc):
    return 16 * (cg % 2) + 4 * (cg // 2) + cc


def fno_layout(x, p_w, p_b, fw, w1_w, w1_b, w2_w, w2_b, q1_w, q1_b, q2_w, q2_b):
    f32 = np.float32
    o = {}
    img = x[..., 0]
    o["image_y"] = img.reshape(IGROUPS, GI, S, S).transpose(0, 3, 1, 2)
    lin = np.linspace(0.0, 1.0, S, dtype=f32)
    feat = np.ones((4, 2, 32, NB, S), f32)
    feat[0] = img.transpose(2, 0, 1).reshape(2, 32, NB, S)
    feat[1] = lin
    feat[2] = lin.reshape(2, 32, 1, 1)
    o["features"] = feat.reshape(4, 2, 32, IGROUPS, GI * S).transpose(3, 0, 2, 1, 4).reshape(IGROUPS, P, 2 * GI * S)
    p = np.concatenate([p_w, p_b[:, None]], 1).T
    lift = np.zeros((4, KQ, KQ, CH), f32)
    for k in range(KQ):
        lift[:, k, k] = p
    o["lift"] = lift.reshape(16, P)
    o["lift_rep"] = np.repeat(p.T[:, :, None], 32, 2).reshape(CH, P)
    w = fw.reshape(LAYERS, 2, CH, CH, M1, KYG, KQ, 2)
    o["modes"] = w.transpose(0, 6, 3, 5, 1, 4, 7, 2).reshape(LAYERS, P, KYG * KX * 2 * CH)
    bd = np.zeros((2, LAYERS, KQ, CH, KQ, CH), f32)
    for k in range(KQ):
        bd[0, :, k, :, k] = w1_w.transpose(0, 2, 1)
        bd[1, :, k, :, k] = w2_w.transpose(0, 2, 1)
    o["w1_blocks"] = bd[0].reshape(LAYERS, P, P)
    o["w2_blocks"] = bd[1].reshape(LAYERS, P, P)
    b1 = np.zeros((LAYERS, 4, 32, 8), f32)
    w2r = np.zeros((LAYERS, CH, 8, 4, 32), f32)
    for cg in range(8):
        for cc in range(4):
            b1[:, cc, :, cg] = w1_b[:, channel(cg, cc), None]
            w2r[:, :, cg, cc] = w2_w[:, :, channel(cg, cc), None]
    o["b1_rep"] = b1.reshape(LAYERS, P, 8)
    o["w2_rep"] = w2r.reshape(LAYERS, CH, 8 * P)
    o["b2_cols"] = w2_b.T
    o["b2_each"] = w2_b[:, :, None]
    o["q1_t"] = q1_w.T
    o["q1_rep"] = np.repeat(q1_w.T[:, :, None], 32, 2).reshape(CH, P)
    o["q1_b_rep"] = np.repeat(q1_b, 32)[:, None]
    o["q2_rep"] = np.repeat(q2_w[0], 32)[:, None]
    o["q2_b_rep"] = np.repeat(q2_b, P)[:, None]
    return {k: np.ascontiguousarray(v) for k, v in o.items()}


def fno(t, d, beside):
    nc = t.nc
    with ExitStack() as ctx:
        sb = lambda name, shape: t.sb("f_" + name, shape, ctx=ctx)
        const = {k: sb(k, d[k].shape) for k in ("to_x", "to_y", "from_y", "from_y1", "from_x", "eye32", "lift", "lift_rep", "b2_cols", "q1_t", "q1_rep", "q1_b_rep", "q2_rep", "q2_b_rep")}
        NM = KYG * KX * 2
        spec = sb("spec", [P, KYG, KX, 2, GI])
        wm = sb("wm", [P, KYG, KX, 4, CH])
        vv = sb("vv", [P, 2, 2, 16, 96])
        bb = sb("bb", [P, GI, 4, 96])
        aa = sb("aa", [96, 8, CHUNK * S])
        rr = sb("rr", [P, 4, 512])
        dd = wm[:].rearrange("p a b c e -> p (a b c e)")[:, 0:4 * 2 * KYG * P].rearrange("p (b r k m) -> p b r k m", b=4, r=2, k=KYG)
        qa = sb("qa", [P, 2, GI * S])
        proj = sb("proj", [P, 8, 4, 32])
        proj_s = sb("proj_s", [P, 8, 4])
        w1b = sb("w1b", [P, P])
        w2b = sb("w2b", [P, P])
        w2r = sb("w2r", [CH, 8 * P])
        b1r = sb("b1r", [P, 8])
        b2e = sb("b2e", [CH, 1])
        qb = sb("qb", [P, 1])
        b2s = sb("b2s", [CH, 1])
        head = sb("head", [P, 32])
        fb = vv[:].rearrange("p a b c e -> p (a b c e)")[:, 0:NM * GI]
        spec_f = spec[:].rearrange("p a b c e -> p (a b c e)")
        loaded = t.sem("f_loaded")
        with t.stage("f_loaded", "own", "ready", "done") as (block, loaded, own, ready, done):
            @block.sync
            def _(sp):
                for k, s in const.items():
                    sp.dma_start(s[:], d[k]).then_inc(loaded, 16)
                sp.wait_ge(loaded, 16 * len(const))

            @block.vector
            def _(v):
                c = Chain(v, own)
                v.wait_ge(loaded, 16 * len(const))
                v.tensor_reduce(b2s[:], const["b2_cols"][:], AX, ALU.add).then_inc(ready, 1)
                c.link(v.tensor_scalar(head[:], const["eye32"][:], const["q2_rep"][:, 0:1], None, ALU.mult))
                v.wait_ge(done, 1)
                c.link(v.tensor_tensor(qb[:], t.bank[0][:, 0:1], const["q1_b_rep"][:], ALU.add))

            @block.tensor
            def _(pe):
                pe.wait_ge(ready, 1)
                pe.matmul(t.bank[0][:, 0:1], const["q1_rep"][:], b2s[:], start=True, stop=True).then_inc(done, 1)

        def build_projection(c, v, n):
            c.link(v.tensor_copy(proj_s[:, 0:n, :], t.bank[7][:, 0:4 * n].rearrange("p (c o) -> p c o", o=4)))
            for j in range(n):
                last = v.tensor_tensor(proj[:, j], const["eye32"][:].unsqueeze(1).broadcast_to([P, 4, 32]), bc(proj_s[:, j, :], 32), ALU.mult)
            return last

        with nc.Fori(0, IGROUPS) as gi:
            xi = bb[0:S, :, :, :].rearrange("p a b c -> p (a b c)")[:, 0:GI * S]
            feat = bb[:].rearrange("p a b c -> p (a b c)")[:, GI * S:3 * GI * S]
            x16 = fb[0:16, :]
            d0 = rr[:].rearrange("p a b -> p (a b)")[:, 0:PAIRS * 24].rearrange("p (b r k q) -> p b r k q", r=2, k=KYG, q=KQ)
            with t.stage("f_loaded", "own", "done", "moved", "x_done", "x_moved", "u_done", "u_moved", "p_done", "p_ready", "q_done", "q_moved") as \
                    (block, loaded, own, done, moved, x_done, x_moved, u_done, u_moved, p_done, p_ready, q_done, q_moved):
                @block.sync
                def _(sp):
                    sp.dma_start(xi, d["image_y"][bass.ds(gi, 1)].rearrange("a y b x -> y (a b x)")).then_inc(loaded, 16)
                    sp.dma_start(x16, d["grid_spectrum"]).then_inc(loaded, 16)
                    sp.dma_start(feat, d["features"][bass.ds(gi, 1)].rearrange("a p n -> p (a n)")).then_inc(loaded, 16)
                    sp.wait_ge(loaded, 48)

                @block.tensor
                def _(pe):
                    pe.wait_ge(loaded, 48)
                    for b in range(PAIRS):
                        last = pe.matmul(t.bank[0][:, b * 24:(b + 1) * 24], xi[:, b * P:(b + 1) * P], const["from_y1"][:], start=True, stop=True)
                    last.then_inc(done, 1)
                    pe.wait_ge(moved, 1)
                    for b in range(PAIRS):
                        if b >= 2:
                            pe.wait_ge(x_moved, b - 1)
                        for k in range(KYG):
                            for r in range(2):
                                last = pe.matmul(t.bank[1 + b % 2][0:4, k * 96:(k + 1) * 96], d0[:, b, r, k, :], const["from_x"][:, r * 96:(r + 1) * 96], start=(r == 0), stop=(r == 1))
                        last.then_inc(x_done, 1)
                    pe.wait_ge(x_moved, PAIRS)
                    for n in range(NM * GI // 512):
                        if n >= 2:
                            pe.wait_ge(u_moved, n - 1)
                        pe.matmul(t.bank[3 + n % 2][:, :], const["lift"][:], x16[:, n * 512:(n + 1) * 512], start=True, stop=True).then_inc(u_done, 1)
                    pe.matmul(t.bank[7][:, 0:4], const["lift_rep"][:], const["q1_t"][:], start=True, stop=True).then_inc(p_done, 1)
                    pe.wait_ge(p_ready, 1)
                    for n in range(8):
                        if n >= 2:
                            pe.wait_ge(q_moved, n - 1)
                        pe.matmul(t.bank[5 + n % 2][:, :], proj[:, 0].rearrange("p o y -> p (o y)"), feat[:, n * 512:(n + 1) * 512], start=True, stop=True).then_inc(q_done, 1)

                @block.vector
                def _(v):
                    c = Chain(v, own)
                    v.wait_ge(done, 1)
                    v.tensor_copy(d0.rearrange("p b r k q -> p (b r k q)"), t.bank[0][:, 0:PAIRS * 24]).then_inc(moved, 1)
                    for b in range(PAIRS):
                        v.wait_ge(x_done, b + 1)
                        dst = x16[0:4, :].rearrange("p (k m b) -> p k m b", k=KYG, b=GI)[:, :, :, 2 * b:2 * b + 2]
                        v.tensor_copy(dst, t.bank[1 + b % 2][0:4, 0:288].rearrange("p (k m b) -> p k m b", k=KYG, b=2)).then_inc(x_moved, 1)
                    for n in range(NM * GI // 512):
                        v.wait_ge(u_done, n + 1)
                        v.tensor_copy(spec_f[:, n * 512:(n + 1) * 512], t.bank[3 + n % 2][:, :]).then_inc(u_moved, 1)
                    v.wait_ge(p_done, 1)
                    build_projection(c, v, 1).then_inc(p_ready, 1)
                    for n in range(8):
                        v.wait_ge(q_done, n + 1)
                        v.tensor_copy(qa[:].rearrange("p a b -> p (a b)")[:, n * 512:(n + 1) * 512], t.bank[5 + n % 2][:, :]).then_inc(q_moved, 1)

            def layer(l, last_layer):
                raw = bb[:].rearrange("p a b c -> p (a b c)")[:, 0:NM * CH]
                NW = NM * CH // 512
                with t.stage("f_loaded", "own", "w_done", "w_turned", "s_done") as (block, loaded, own, w_done, w_turned, s_done):
                    @block.sync
                    def _(sp):
                        at = (lambda a: a[l]) if isinstance(l, int) else (lambda a: a[bass.ds(l, 1)].squeeze(0))
                        for dst, k in ((raw, "modes"), (w1b[:], "w1_blocks"), (w2b[:], "w2_blocks"), (w2r[:], "w2_rep"), (b1r[:], "b1_rep"), (b2e[:], "b2_each")):
                            sp.dma_start(dst, at(d[k])).then_inc(loaded, 16)
                        sp.wait_ge(loaded, 96)

                    @block.tensor
                    def _(pe):
                        pe.wait_ge(loaded, 96)
                        for n in range(NW):
                            if n >= 4:
                                pe.wait_ge(w_turned, n - 3)
                            pe.matmul(t.bank[n % 4][:, :], w1b[:], raw[:, n * 512:(n + 1) * 512], start=True, stop=True).then_inc(w_done, 1)
                        for j in range(8):
                            last = pe.matmul(t.bank[7][:, 4 * j:4 * j + 4], w2r[:, j * P:(j + 1) * P], const["q1_t"][:], start=True, stop=True)
                        last.then_inc(s_done, 1)

                    @block.vector
                    def _(v):
                        c = Chain(v, own)
                        for n in range(NW):
                            v.wait_ge(w_done, n + 1)
                            kg, k8 = n // 3, n % 3
                            dst = wm[:, kg, k8 * 8:(k8 + 1) * 8, 1:3, :]
                            for k in range(8):
                                last = v.transpose(dst[:, k].rearrange("p r o -> p (r o)"), t.bank[n % 4][:, k * 64:(k + 1) * 64])
                            last.then_inc(w_turned, 1)
                        v.wait_ge(s_done, 1)
                        c.link(build_projection(c, v, 8))

                    @block.scalar
                    def _(act):
                        act.wait_ge(w_turned, NW)
                        act.activation(wm[:, :, :, 0, :].rearrange("p a b c -> p (a b) c"), wm[:, :, :, 2, :].rearrange("p a b c -> p (a b) c"), ACT.Copy, scale=-1.0)
                        act.activation(wm[:, :, :, 3, :].rearrange("p a b c -> p (a b) c"), wm[:, :, :, 1, :].rearrange("p a b c -> p (a b) c"), ACT.Copy, scale=-1.0)
                for half in range(2):
                    with t.stage("x_done", "x_moved", "x_moved_v") as (block, x_done, x_moved, x_moved_v):
                        @block.tensor
                        def _(pe):
                            for k4 in range(KX // 4):
                                if k4 >= 2:
                                    pe.wait_ge(x_moved, k4 - 1)
                                    pe.wait_ge(x_moved_v, k4 - 1)
                                for j in range(4):
                                    kx = k4 * 4 + j
                                    for r in range(2):
                                        for kg in range(KYG):
                                            for q in range(2):
                                                kq = 2 * half + q
                                                rows = slice(32 * kq, 32 * kq + 32)
                                                out = t.bank[2 * (k4 % 2) + q][32 * kg:32 * kg + 32, :].rearrange("p (r o m) -> p r m o", r=2, m=16)[:, :, 4 * j:4 * j + 4, :]
                                                w = wm[rows, kg, kx].rearrange("p a o -> p (a o)")
                                                lo = (1 - r) * CH
                                                first = w[:, lo:lo + 2 * CH]
                                                rhs = bass.AP(first.tensor, first.offset, [list(first.ap[0]), [CH, 2], [16, 4], [1, 16]])
                                                last = pe.matmul(out, spec[rows, kg, kx, r, :], rhs, start=(r == 0), stop=(r == 1), skip_group_check=True)
                                last.then_inc(x_done, 1)

                        def move(eng, k4, q):
                            dst = vv[0:96, q].rearrange("p r o m -> p (r o) m")[:, :, k4 * 16:(k4 + 1) * 16]
                            return dst, t.bank[2 * (k4 % 2) + q][0:96, :].rearrange("p (c m) -> p c m", m=16)

                        @block.scalar
                        def _(act):
                            for k4 in range(KX // 4):
                                act.wait_ge(x_done, k4 + 1)
                                act.activation(*move(act, k4, 0), ACT.Copy).then_inc(x_moved, 1)

                        @block.vector
                        def _(v):
                            for k4 in range(KX // 4):
                                v.wait_ge(x_done, k4 + 1)
                                v.tensor_copy(*move(v, k4, 1)).then_inc(x_moved_v, 1)
                    with t.stage("x_done", "x_moved", "x_moved_v") as (block, x_done, x_moved, x_moved_v):
                        @block.tensor
                        def _(pe):
                            for n in range(16):
                                q, rot, c2 = n // 8, n // 4 % 2, n % 4
                                if n >= 4:
                                    pe.wait_ge(x_moved if n % 2 == 0 else x_moved_v, (n - 4) // 2 + 1)
                                for c1 in range(4):
                                    last = pe.transpose(t.bank[4 + n % 4][0:96, c1 * 96:(c1 + 1) * 96], vv[0:96, q, rot, c2 * 4 + c1, :], t.ident[0:96, 0:96])
                                last.then_inc(x_done, 1)

                        def place(n):
                            q, rot, c2 = n // 8, n // 4 % 2, n % 4
                            kq = 2 * half + q
                            dst = bb[0:96, :, c2, :].rearrange("p b (c k g r) -> p k r c g b", c=4, k=KQ, g=KYG)[:, kq, rot]
                            return dst, t.bank[4 + n % 4][0:96, 0:384].rearrange("p (c g b) -> p c g b", c=4, g=KYG)

                        @block.scalar
                        def _(act):
                            for n in range(0, 16, 2):
                                act.wait_ge(x_done, n + 1)
                                act.activation(*place(n), ACT.Copy).then_inc(x_moved, 1)

                        @block.vector
                        def _(v):
                            for n in range(1, 16, 2):
                                v.wait_ge(x_done, n + 1)
                                v.tensor_copy(*place(n)).then_inc(x_moved_v, 1)
                for ch in range(CHUNKS):
                    with t.stage("a_done", "a_moved", "f_loaded") as (block, a_done, a_moved, loaded):
                        @block.sync
                        def _(sp):
                            beside.fetch(sp, gi * (LAYERS * CHUNKS) + l * CHUNKS + ch, loaded)
                            sp.wait_ge(loaded, 32)

                        @block.tensor
                        def _(pe):
                            for b in range(CHUNK):
                                if b >= 2:
                                    pe.wait_ge(a_moved, b - 1)
                                for c2 in range(4):
                                    last = pe.matmul(t.bank[b % 2][0:96, c2 * P:(c2 + 1) * P], bb[0:96, ch * CHUNK + b, c2, :], const["to_x"][:], start=True, stop=True)
                                last.then_inc(a_done, 1)

                        @block.scalar
                        def _(act):
                            for b in range(CHUNK):
                                act.wait_ge(a_done, b + 1)
                                act.activation(aa[:, :, b * S:(b + 1) * S], t.bank[b % 2][0:96, :].rearrange("p (c x) -> p c x", x=S), ACT.Copy).then_inc(a_moved, 1)
                    with t.stage("y_done", "r_done", "r_done_v", "f_done", "f_moved", "p_done", "pool_sent") as (block, y_done, r_done, r_done_v, f_done, f_moved, p_done, scattered):
                        @block.gpsimd
                        def _(p):
                            beside.send(p, scattered)

                        @block.tensor
                        def _(pe):
                            def use(cg):
                                pe.wait_ge(r_done, cg + 1)
                                pe.wait_ge(r_done_v, cg + 1)
                                for hf in range(2):
                                    last = pe.matmul(t.bank[4 + hf][:, :], proj[:, cg].rearrange("p o y -> p (o y)"), rr[:, cg % 2 * 2 + hf, :], start=(cg == 0), stop=(cg == 7))
                                if cg == 7:
                                    last.then_inc(p_done, 1)
                                if last_layer:
                                    if cg < 7:
                                        last.then_inc(f_done, 1)
                                    return
                                if cg >= 2:
                                    pe.wait_ge(f_moved, cg - 1)
                                for b in range(4):
                                    for hf in range(2):
                                        last = pe.matmul(t.bank[6 + cg % 2][:, b * 96:(b + 1) * 96], rr[:, cg % 2 * 2 + hf, b * P:(b + 1) * P], const["from_y"][:, hf * 96:(hf + 1) * 96], start=(hf == 0), stop=(hf == 1))
                                last.then_inc(f_done, 1)
                            for cg in range(8):
                                if cg >= 2:
                                    pe.wait_ge(r_done, cg - 1)
                                    pe.wait_ge(r_done_v, cg - 1)
                                for hf in range(2):
                                    last = pe.matmul(t.bank[cg % 2 * 2 + hf][:, :], const["to_y"][:, hf * P:(hf + 1) * P], aa[:, cg, :], start=True, stop=True)
                                last.then_inc(y_done, 1)
                                if cg >= 1:
                                    use(cg - 1)
                            use(7)

                        @block.scalar
                        def _(act):
                            def spread(cg):
                                act.wait_ge(f_done, cg + 1)
                                n0 = channel(cg, 0)
                                dst = dd.rearrange("p b r k m -> p b (r k m)").rearrange("p b (f c) -> p b f c", c=CH)[:, :, :, n0:n0 + 4]
                                act.activation(dst, t.bank[6 + cg % 2][:, 0:384].rearrange("p (b f c) -> p b f c", b=4, c=4), ACT.Copy).then_inc(f_moved, 1)
                            for cg in range(8):
                                act.wait_ge(y_done, cg + 1)
                                if cg >= 2:
                                    act.wait_ge(f_done, cg - 1)
                                act.activation(rr[:, cg % 2 * 2, :], t.bank[cg % 2 * 2][:, :], ACT.Relu, bias=b1r[:, cg:cg + 1]).then_inc(r_done, 1)
                                if cg >= 1 and not last_layer:
                                    spread(cg - 1)
                            if not last_layer:
                                spread(7)

                        @block.vector
                        def _(v):
                            for cg in range(8):
                                v.wait_ge(y_done, cg + 1)
                                if cg >= 2:
                                    v.wait_ge(f_done, cg - 1)
                                v.tensor_scalar(rr[:, cg % 2 * 2 + 1, :], t.bank[cg % 2 * 2 + 1][:, :], b1r[:, cg:cg + 1], 0.0, ALU.add, ALU.max).then_inc(r_done_v, 1)
                            v.wait_ge(p_done, 1)
                            for hf in range(2):
                                q = qa[:, hf, ch * 512:(ch + 1) * 512]
                                v.tensor_tensor(q, q, t.bank[4 + hf][:, :], ALU.add)
                    if last_layer:
                        continue
                    with t.stage("x_done", "x_moved") as (block, x_done, x_moved):
                        @block.tensor
                        def _(pe):
                            for b in range(4):
                                if b >= 2:
                                    pe.wait_ge(x_moved, b - 1)
                                for k in range(KYG):
                                    for r in range(2):
                                        last = pe.matmul(t.bank[b % 2][:, k * 96:(k + 1) * 96], dd[:, b, r, k, :], const["from_x"][:, r * 96:(r + 1) * 96], start=(r == 0), stop=(r == 1))
                                last.then_inc(x_done, 1)

                        @block.vector
                        def _(v):
                            for b in range(4):
                                v.wait_ge(x_done, b + 1)
                                i0 = ch * CHUNK + 2 * b
                                dst = fb.rearrange("p (k m b) -> p k m b", k=KYG, b=GI)[:, :, :, i0:i0 + 2]
                                v.tensor_copy(dst, t.bank[b % 2][:, 0:288].rearrange("p (k m b) -> p k m b", k=KYG, b=2)).then_inc(x_moved, 1)
                if last_layer:
                    return
                with t.stage("u_done", "u_moved", "own") as (block, u_done, u_moved, own):
                    @block.tensor
                    def _(pe):
                        for n in range(NM * GI // 512):
                            if n >= 2:
                                pe.wait_ge(u_moved, n - 1)
                            pe.matmul(t.bank[n % 2][:, :], w2b[:], fb[:, n * 512:(n + 1) * 512], start=True, stop=True).then_inc(u_done, 1)

                    @block.vector
                    def _(v):
                        c = Chain(v, own)
                        for n in range(NM * GI // 512):
                            v.wait_ge(u_done, n + 1)
                            u = spec_f[:, n * 512:(n + 1) * 512]
                            v.tensor_tensor(u, u, t.bank[n % 2][:, :], ALU.add).then_inc(u_moved, 1)
                        c.link(v.tensor_scalar(b2e[:], b2e[:], float(S), None, ALU.mult))
                        v.wait_ge(u_moved, NM * GI // 512)
                        dc = spec[0:CH, 0, 0, 0, :]
                        c.link(v.tensor_scalar(dc, dc, b2e[:, 0:1], None, ALU.add))

            with nc.Fori(0, LAYERS - 1) as l:
                layer(l, False)
            layer(LAYERS - 1, True)
            with t.stage("own", "relu_done", "o_done") as (block, own, relu_done, o_done):
                @block.scalar
                def _(act):
                    for hf in range(2):
                        act.activation(qa[:, hf, :], qa[:, hf, :], ACT.Relu, bias=qb[:, 0:1]).then_inc(relu_done, 1)

                @block.tensor
                def _(pe):
                    pe.wait_ge(relu_done, 2)
                    for b in range(PAIRS):
                        for hf in range(2):
                            last = pe.matmul(t.bank[b // 8][:, b % 8 * D + hf * 32:b % 8 * D + hf * 32 + 32], qa[:, hf, b * P:(b + 1) * P], head[:], start=True, stop=True)
                    last.then_inc(o_done, 1)

                @block.vector
                def _(v):
                    v.wait_ge(o_done, 1)
                    for n in range(2):
                        v.tensor_scalar(t.h[:, bass.ds(gi * PAIRS + n * 8, 8), :], t.bank[n][:, :].rearrange("p (k d) -> p k d", d=D), const["q2_b_rep"][:, 0:1], None, ALU.add)


def norm_stage(t, src, dst, eps, centre=True, gain=None, shift=None, add_src=False):
    nc, n = t.nc, src.shape[1]
    mean, var, tmp = t.n_mean[:, 0:n], t.n_var[:, 0:n], t.n_tmp[:, 0:n, :]
    with t.stage("own", "centred", "squared", "var_ready", "std_ready") as (block, own, centred, squared, var_ready, std_ready):
        base = dst if centre else src

        @block.vector
        def _(v):
            c = Chain(v, own)
            if centre:
                c.link(v.tensor_reduce(mean, src, AX, ALU.add))
                c.link(v.tensor_scalar(mean, mean, -1.0 / D, None, ALU.mult))
                v.tensor_tensor(dst, src, bc(mean, D), ALU.add).then_inc(centred, 1)
            v.wait_ge(squared, 1)
            c.link(v.tensor_reduce(var, tmp, AX, ALU.add))
            v.tensor_scalar(var, var, 1.0 / D, eps, ALU.mult, ALU.add).then_inc(var_ready, 1)
            v.wait_ge(std_ready, 1)
            c.link(v.reciprocal(mean, var))
            c.link(v.tensor_tensor(dst, base, bc(mean, D), ALU.mult))
            if gain is not None:
                c.link(v.tensor_tensor(dst, dst, gain.unsqueeze(1).broadcast_to([P, n, D]), ALU.mult))
            if shift is not None:
                c.link(v.tensor_tensor(dst, dst, shift.unsqueeze(1).broadcast_to([P, n, D]), ALU.add))
            if add_src:
                c.link(v.tensor_tensor(dst, dst, src, ALU.add))

        @block.scalar
        def _(act):
            if centre:
                act.wait_ge(centred, 1)
            act.activation(tmp, base, ACT.Square).then_inc(squared, 1)
            act.wait_ge(var_ready, 1)
            act.activation(var, var, ACT.Sqrt).then_inc(std_ready, 1)


def turn_stage(t, src, dst):
    nc = t.nc
    with t.stage("turned", "moved") as (block, turned, moved):
        G = src.shape[1] // GT

        @block.tensor
        def _(pe):
            for g in range(G):
                if g >= 2:
                    pe.wait_ge(moved, g - 1)
                for k in range(GT):
                    last = pe.transpose(t.bank[g % 2][0:D, k * P:(k + 1) * P], src[:, g * GT + k, :], t.ident[:, :])
                last.then_inc(turned, 1)

        @block.scalar
        def _(act):
            for g in range(G):
                act.wait_ge(turned, g + 1)
                act.activation(dst[0:D, g * 512:(g + 1) * 512], t.bank[g % 2][0:D, :], ACT.Copy).then_inc(moved, 1)


def l0_attention(t, q_w):
    nc = t.nc
    with ExitStack() as ctx:
        x = t.sb("a0_x", [P, IT, D], ctx=ctx)
        xt = t.sb("a0_xt", [D + 1, IT * P], ctx=ctx)
        qt = t.sb("a0_qt", [D, 2, 512], ctx=ctx)
        att = t.sb("a0_att", [P, 2, GT, P], ctx=ctx)
        with t.stage("z") as (block, z):
            @block.vector
            def _(v):
                v.memset(att[:], 0.0)
        with nc.Fori(0, STEPS) as it:
            h = t.h[:, bass.ds(it * IT, IT), :]
            norm_stage(t, h, x[:], 1e-5)
            turn_stage(t, x, xt)
            with t.stage("q_done", "q_moved", "s_done", "a_ready", "v_done", "h_added") as (block, q_done, q_moved, s_done, a_ready, v_done, h_added):
                @block.tensor
                def _(pe):
                    def values(g):
                        pe.wait_ge(a_ready, g + 1)
                        if g >= 2:
                            pe.wait_ge(h_added, g - 1)
                        for k in range(GT):
                            last = pe.matmul(t.bank[4 + g % 2][:, k * D:(k + 1) * D], att[:, g % 2, k, :], x[:, g * GT + k, :], start=True, stop=True)
                        last.then_inc(v_done, 1)
                    for g in range(G):
                        if g >= 2:
                            pe.wait_ge(q_moved, g - 1)
                        pe.matmul(t.bank[g % 2][0:D, :], q_w, xt[0:D, g * 512:(g + 1) * 512], start=True, stop=True).then_inc(q_done, 1)
                        pe.wait_ge(q_moved, g + 1)
                        if g >= 2:
                            pe.wait_ge(a_ready, g - 1)
                        for k in range(GT):
                            tok = slice(g * 512 + k * P, g * 512 + (k + 1) * P)
                            last = pe.matmul(t.bank[2 + g % 2][:, k * P:(k + 1) * P], xt[0:D, tok], qt[:, g % 2, k * P:(k + 1) * P], start=True, stop=True)
                        last.then_inc(s_done, 1)
                        if g >= 1:
                            values(g - 1)
                    values(G - 1)

                @block.scalar
                def _(act):
                    for g in range(G):
                        if g >= 2:
                            act.wait_ge(v_done, g - 1)
                        act.wait_ge(s_done, g + 1)
                        for hf in range(2):
                            r = slice(hf * S, hf * S + S)
                            sc = t.bank[2 + g % 2][r, :].rearrange("p (k c) -> p k c", c=P)[:, :, r]
                            last = act.activation(att[r, g % 2, :, r], sc, ACT.Sigmoid)
                        last.then_inc(a_ready, 1)

                @block.vector
                def _(v):
                    def add(g):
                        v.wait_ge(v_done, g + 1)
                        hg = t.h[:, bass.ds(it * IT + g * GT, GT), :]
                        v.tensor_tensor(hg, hg, t.bank[4 + g % 2][:, 0:GT * D].rearrange("p (k d) -> p k d", d=D), ALU.add).then_inc(h_added, 1)
                    for g in range(G):
                        v.wait_ge(q_done, g + 1)
                        if g >= 2:
                            v.wait_ge(s_done, g - 1)
                        v.tensor_copy(qt[:, g % 2, :], t.bank[g % 2][0:D, :]).then_inc(q_moved, 1)
                        if g >= 1:
                            add(g - 1)
                    add(G - 1)



def experts(t, name, x, xt, gate_t, E, F, act_fn, w1, w2, b2, acc, gates, base):
    nc = t.nc
    units = E * F // P
    per = max(1, F // P)
    pair = max(1, P // F)
    steps = units // per
    HR = 2 * per + 1
    with ExitStack() as ctx:
        hid = t.sb(name + "_hid", [P, HR, 512], ctx=ctx)
        with t.stage("g_turned", "g_moved", "b_done", "u_done", "u_moved", "y_done", "y_used", "acc0") as \
                (block, g_turned, g_moved, b_done, u_done, u_moved, y_done, y_used, acc0):
            def hbank(n):
                return t.bank[n % 3]

            YR = 3 if pair == 1 else 2

            def ybank(n, q):
                return t.bank[3 + n % 3] if pair == 1 else t.bank[3 + n % 2 * 2 + q]

            @block.tensor
            def _(pe):
                for g in range(G):
                    if g >= 1:
                        pe.wait_ge(g_moved, g)
                    for k in range(GT):
                        last = pe.transpose(t.bank[6][0:E, k * P:(k + 1) * P], gates[:, g * GT + k, :], t.ident[:, :])
                    last.then_inc(g_turned, 1)
                for g in range(G):
                    pe.wait_ge(g_moved, g + 1)
                    if g >= 1:
                        pe.wait_ge(acc0, g)
                    for k in range(GT):
                        last = pe.matmul(t.bank[7][:, k * D:(k + 1) * D], gate_t[0:E, g * 512 + k * P:g * 512 + (k + 1) * P], b2[0:E, :], start=True, stop=True)
                    last.then_inc(b_done, 1)

                def second(n):
                    g, s = n // steps, n % steps
                    pe.wait_ge(u_moved, (n + 1) * per)
                    if n >= YR:
                        pe.wait_ge(y_used, n - YR + 1)
                    for q in range(pair):
                        r = slice(q * F, (q + 1) * F) if pair > 1 else slice(0, P)
                        for k in range(GT):
                            for j in range(per):
                                u = n * per + j
                                last = pe.matmul(ybank(n, q)[:, k * D:(k + 1) * D], hid[r, u % HR, k * P:(k + 1) * P],
                                                 w2[r, s * per + j, :], start=(j == 0), stop=(j == per - 1))
                    last.then_inc(y_done, 1)

                for n in range(G * steps):
                    g, s = n // steps, n % steps
                    for j in range(per):
                        u = n * per + j
                        if u >= 3:
                            pe.wait_ge(u_moved, u - 2)
                        m = s * per + j
                        pe.matmul(hbank(u)[:, :], w1[0:D + 1, m * P:(m + 1) * P], xt[0:D + 1, g * 512:(g + 1) * 512], start=True, stop=True).then_inc(u_done, 1)
                    if n >= 1:
                        second(n - 1)
                second(G * steps - 1)

            @block.scalar
            def _(act):
                for g in range(G):
                    act.wait_ge(g_turned, g + 1)
                    act.activation(gate_t[0:E, g * 512:(g + 1) * 512], t.bank[6][0:E, :], ACT.Copy).then_inc(g_moved, 1)
                for u in range(G * units):
                    act.wait_ge(u_done, u + 1)
                    if u >= HR:
                        act.wait_ge(y_done, (u - HR) // per + 1)
                    act.activation(hid[:, u % HR, :], hbank(u)[:, :], act_fn).then_inc(u_moved, 1)

            @block.vector
            def _(v):
                for g in range(G):
                    v.wait_ge(b_done, g + 1)
                    a = acc[:, g * GT:(g + 1) * GT, :]
                    b = t.bank[7][:, 0:GT * D].rearrange("p (k d) -> p k d", d=D)
                    if base is None:
                        v.tensor_copy(a, b).then_inc(acc0, 1)
                    else:
                        v.tensor_tensor(a, b, base[:, g * GT:(g + 1) * GT, :], ALU.add).then_inc(acc0, 1)
                v.wait_ge(acc0, G)
                for n in range(G * steps):
                    g, s = n // steps, n % steps
                    v.wait_ge(y_done, n + 1)
                    for q in range(pair):
                        if n or q:
                            v.wait_ge(y_used, n) if q == 0 else v.wait_ge(t.sem("y_half"), n + 1)
                        for k in range(GT):
                            e = s * pair + q
                            a = acc[:, g * GT + k, :]
                            last = v.scalar_tensor_tensor(a, ybank(n, q)[:, k * D:(k + 1) * D], gates[:, g * GT + k, e:e + 1], a, ALU.mult, ALU.add)
                        if q < pair - 1:
                            last.then_inc(t.sem("y_half"), 1)
                    last.then_inc(y_used, 1)
        if pair > 1:
            nc.gpsimd.sem_clear(t.sem("y_half"))
            nc.all_engine_barrier()


def logits_stage(t, xt, gw, E, out):
    with t.stage("l_done") as (block, l_done):
        @block.tensor
        def _(pe):
            for k in range(IT):
                last = pe.matmul(t.bank[0][:, k * E:(k + 1) * E], xt[:, k * P:(k + 1) * P], gw, start=True, stop=True)
            last.then_inc(l_done, 1)

        @block.vector
        def _(v):
            v.wait_ge(l_done, 1)
            v.tensor_copy(out, t.bank[0][:, 0:IT * E].rearrange("p (k e) -> p k e", e=E))


def exp_rows(t, lg, key, total, n, e):
    with t.stage("own", "shifted", "exped") as (block, own, shifted, exped):
        @block.vector
        def _(v):
            c = Chain(v, own)
            c.link(v.tensor_reduce(key, lg, AX, ALU.max))
            v.tensor_tensor(lg, lg, bc(key, e), ALU.subtract).then_inc(shifted, 1)
            v.wait_ge(exped, 1)
            c.link(v.tensor_reduce(total, lg, AX, ALU.add))
            c.link(v.reciprocal(total, total))

        @block.scalar
        def _(act):
            act.wait_ge(shifted, 1)
            act.activation(lg, lg, ACT.Exp).then_inc(exped, 1)


def pick_first(c, v, t, val, key, pick, tmp, e):
    n = val.shape[1]
    order = t.falling[0:val.shape[0], 0:e].unsqueeze(1).broadcast_to([val.shape[0], n, e])
    c.link(v.tensor_reduce(key, val, AX, ALU.max))
    c.link(v.tensor_tensor(pick, val, bc(key, e), ALU.is_equal))
    c.link(v.tensor_tensor(pick, pick, order, ALU.mult))
    c.link(v.tensor_reduce(tmp, pick, AX, ALU.max))
    c.link(v.tensor_tensor(pick, pick, bc(tmp, e), ALU.is_equal))


def l0_experts(t, gw, w1, w2, b2):
    nc, E, F = t.nc, 8, 256
    cap = float(-(-5 * NB * S // (4 * E)))
    with ExitStack() as ctx:
        x = t.sb("e0_x", [P, IT, D], ctx=ctx)
        acc = t.sb("e0_acc", [P, IT, D], ctx=ctx)
        tmp = t.sb("e0_tmp", [P, IT, D], ctx=ctx)
        xt = t.sb("e0_xt", [D + 1, IT * P], ctx=ctx)
        gate_t = t.sb("e0_gt", [E, IT * P], ctx=ctx)
        lg = t.sb("e0_lg", [P, IT, E], ctx=ctx)
        pick = t.sb("e0_pick", [P, IT, E], ctx=ctx)
        seen = t.sb("e0_seen", [P, IT, E], ctx=ctx)
        key = t.sb("e0_key", [P, IT], ctx=ctx)
        tot = t.sb("e0_tot", [P, IT], ctx=ctx)
        one = t.sb("e0_one", [P, IT], ctx=ctx)
        carry = t.sb("e0_carry", [P, E], ctx=ctx)
        with t.stage("z") as (block, z):
            @block.vector
            def _(v):
                v.memset(xt[D:D + 1, :], 1.0)
                v.memset(carry[:], 0.0)
        with nc.Fori(0, STEPS) as it:
            h = t.h[:, bass.ds(it * IT, IT), :]
            norm_stage(t, h, x[:], 1e-5)
            turn_stage(t, x, xt)
            logits_stage(t, xt, gw, E, lg[:])
            exp_rows(t, lg[:], key[:], tot[:], IT, E)
            with t.stage("own", "picked", "counted") as (block, own, picked, counted):
                @block.vector
                def _(v):
                    c = Chain(v, own)
                    pick_first(c, v, t, lg[:], key[:], pick[:], one[:], E)
                    v.tensor_copy(one[:], key[:]).then_inc(picked, 1)
                    v.wait_ge(counted, 1)
                    within = t.bank[0][:, 0:IT * E].rearrange("p (k e) -> p k e", e=E)
                    total = t.bank[1][:, 0:IT * E].rearrange("p (k e) -> p k e", e=E)
                    for e in range(E):
                        last = v.tensor_tensor_scan(seen[:, :, e], total[:, :, e], pick[:, :, e], carry[:, e:e + 1], ALU.add, ALU.bypass)
                    c.link(last)
                    c.link(v.tensor_copy(carry[:], seen[:, IT - 1, :]))
                    c.link(v.tensor_tensor(seen[:], seen[:], total, ALU.subtract))
                    c.link(v.tensor_tensor(seen[:], seen[:], within, ALU.add))
                    c.link(v.tensor_scalar(seen[:], seen[:], cap, None, ALU.is_le))
                    c.link(v.tensor_tensor(seen[:], seen[:], pick[:], ALU.mult))
                    c.link(v.tensor_tensor(seen[:], seen[:], bc(tot[:], E), ALU.mult))

                @block.tensor
                def _(pe):
                    pe.wait_ge(picked, 1)
                    pk = pick[:].rearrange("p k e -> p (k e)")
                    pe.matmul(t.bank[0][:, 0:IT * E], t.upto[:, :], pk, start=True, stop=True)
                    pe.matmul(t.bank[1][:, 0:IT * E], t.ones[:, :], pk, start=True, stop=True).then_inc(counted, 1)
            experts(t, "e0", x, xt, gate_t, E, F, ACT.Relu, w1, w2, b2, acc, seen, None)
            with t.stage("own") as (block, own):
                @block.vector
                def _(v):
                    c = Chain(v, own)
                    big = 3.4028234663852886e38
                    c.link(v.tensor_scalar(tmp[:], acc[:], 0.0, 1e4, ALU.is_gt, ALU.mult))
                    c.link(v.tensor_scalar(x[:], acc[:], 0.0, -1e4, ALU.is_lt, ALU.mult))
                    c.link(v.tensor_tensor(tmp[:], tmp[:], x[:], ALU.add))
                    c.link(v.tensor_scalar(x[:], acc[:], big, None, ALU.is_le))
                    c.link(v.scalar_tensor_tensor(x[:], acc[:], -big, x[:], ALU.is_ge, ALU.mult))
                    c.link(v.copy_predicated(tmp[:], x[:].bitcast(I32), acc[:]))
                    c.link(v.tensor_tensor(h, h, tmp[:], ALU.add))


def top_two(c, v, t, lg, scale, b, out):
    e = lg.shape[2]
    pick_first(c, v, t, lg, b["k1"], b["p1"], b["one"], e)
    c.link(v.scalar_tensor_tensor(out, b["p1"], -4.0, lg, ALU.mult, ALU.add))
    pick_first(c, v, t, out, b["k2"], b["p2"], b["one"], e)


def l1_experts(t, gw, w1, w2, b2):
    nc, E, F = t.nc, 8, 64
    with ExitStack() as ctx:
        x = t.sb("e1_x", [P, IT, D], ctx=ctx)
        acc = t.sb("e1_acc", [P, IT, D], ctx=ctx)
        xt = t.sb("e1_xt", [D + 1, IT * P], ctx=ctx)
        gate_t = t.sb("e1_gt", [E, IT * P], ctx=ctx)
        lg = t.sb("e1_lg", [P, IT, E], ctx=ctx)
        gates = t.sb("e1_gates", [P, IT, E], ctx=ctx)
        b = {k: t.sb("e1_" + k, [P, IT], ctx=ctx)[:] for k in ("k1", "k2", "one", "tot")}
        b |= {k: t.sb("e1_" + k, [P, IT, E], ctx=ctx)[:] for k in ("p1", "p2")}
        with t.stage("z") as (block, z):
            @block.vector
            def _(v):
                v.memset(xt[D:D + 1, :], 1.0)
        with nc.Fori(0, STEPS) as it:
            h = t.h[:, bass.ds(it * IT, IT), :]
            norm_stage(t, h, x[:], 1e-5)
            turn_stage(t, x, xt)
            logits_stage(t, xt[0:D, :], gw[0:D, :], E, lg[:])
            exp_rows(t, lg[:], b["k1"], b["tot"], IT, E)
            with t.stage("own") as (block, own):
                @block.vector
                def _(v):
                    c = Chain(v, own)
                    c.link(v.tensor_tensor(lg[:], lg[:], bc(b["tot"], E), ALU.mult))
                    top_two(c, v, t, lg[:], None, b, gates[:])
                    c.link(v.tensor_tensor(b["tot"], b["k1"], b["k2"], ALU.add))
                    c.link(v.tensor_scalar(b["tot"], b["tot"], 1e-12, None, ALU.max))
                    c.link(v.reciprocal(b["tot"], b["tot"]))
                    c.link(v.tensor_tensor(b["p1"], b["p1"], b["p2"], ALU.add))
                    c.link(v.tensor_tensor(b["p1"], b["p1"], lg[:], ALU.mult))
                    c.link(v.tensor_tensor(gates[:], b["p1"], bc(b["tot"], E), ALU.mult))
            experts(t, "e1", x, xt, gate_t, E, F, ACT.Gelu, w1, w2, b2, acc, gates, x)
            with t.stage("z") as (block, z):
                @block.vector
                def _(v):
                    v.tensor_tensor(h, h, acc[:], ALU.add)


def dense_stage(t, src_t, w, dst, width, base=None, K=D + 1):
    per = 512 // width if width > D else GT
    IT = dst.shape[1]
    with t.stage("m_done", "m_moved") as (block, m_done, m_moved):
        @block.tensor
        def _(pe):
            for g in range(IT // per):
                if g >= 2:
                    pe.wait_ge(m_moved, g - 1)
                for k in range(per):
                    n = g * per + k
                    last = pe.matmul(t.bank[g % 2][:, k * width:(k + 1) * width], src_t[0:K, n * P:(n + 1) * P], w, start=True, stop=True)
                last.then_inc(m_done, 1)

        @block.vector
        def _(v):
            for g in range(IT // per):
                v.wait_ge(m_done, g + 1)
                b = t.bank[g % 2][:, 0:per * width].rearrange("p (k d) -> p k d", d=width)
                if base is None:
                    v.tensor_copy(dst[:, g * per:(g + 1) * per, :], b).then_inc(m_moved, 1)
                else:
                    v.tensor_tensor(dst[:, g * per:(g + 1) * per, :], b, base[:, g * per:(g + 1) * per, :], ALU.add).then_inc(m_moved, 1)


def linear_attention(t, xt, wq, wkv, qt, k, va, out):
    nc = t.nc
    with ExitStack() as ctx:
        low = t.sb("la_low", [P, 2, 512], ctx=ctx)
        ex = t.sb("la_ex", [P, 2, 512], ctx=ctx)
        r = t.sb("la_r", [D, 2, 2 * GT, 2 * D], ctx=ctx)
        den = t.sb("la_den", [P, 2, GT * D], ctx=ctx)
        with t.stage("mm_done", "low_done", "ex_done", "e_used") as (block, mm_done, low_done, ex_done, e_used):
            @block.tensor
            def _(pe):
                for n in range(2 * G):
                    g = n // 2
                    if n >= 3:
                        pe.wait_ge(e_used, n - 2)
                    if n % 2 == 0:
                        last = pe.matmul(t.bank[n % 3][0:D, :], wq, xt[0:D, g * 512:(g + 1) * 512], start=True, stop=True)
                    else:
                        for j in range(GT):
                            last = pe.matmul(t.bank[n % 3][:, j * P:(j + 1) * P], xt[0:D, g * 512 + j * P:g * 512 + (j + 1) * P], wkv, start=True, stop=True)
                    last.then_inc(mm_done, 1)

            def part(n, buf):
                if n % 2 == 0:
                    return buf[0:D, :]
                return buf[:, :].rearrange("p (j c) -> p j c", c=P)[:, :, 0:D]

            def sbuf(n, buf):
                if n % 2 == 0:
                    return buf[0:D, n % 2, :]
                return buf[:, n % 2, 0:GT * D].rearrange("p (j c) -> p j c", c=D)

            @block.vector
            def _(v):
                def finish(n):
                    g = n // 2
                    v.wait_ge(ex_done, n + 1)
                    if n % 2 == 0:
                        dst = qt[0:D, g * 512:(g + 1) * 512]
                    else:
                        dst = k[:, g * GT:(g + 1) * GT, :]
                        v.tensor_copy(va[:, g * GT:(g + 1) * GT, 0:D], t.bank[n % 3][:, :].rearrange("p (j c) -> p j c", c=P)[:, :, D:2 * D])
                    v.scalar_tensor_tensor(dst, part(n, t.bank[n % 3]), 0.0, sbuf(n, ex), ALU.max, ALU.add).then_inc(e_used, 1)
                for n in range(2 * G):
                    v.wait_ge(mm_done, n + 1)
                    if n >= 2:
                        v.wait_ge(ex_done, n - 1)
                    v.tensor_scalar(sbuf(n, low), part(n, t.bank[n % 3]), 0.0, None, ALU.min).then_inc(low_done, 1)
                    if n >= 1:
                        finish(n - 1)
                finish(2 * G - 1)

            @block.scalar
            def _(act):
                for n in range(2 * G):
                    act.wait_ge(low_done, n + 1)
                    if n >= 2:
                        act.wait_ge(e_used, n - 1)
                    act.activation(sbuf(n, ex), sbuf(n, low), ACT.Exp).then_inc(ex_done, 1)
        with t.stage("kv_done", "r_ready", "o_done", "o_used", "own") as (block, kv_done, r_ready, o_done, o_used, own):
            @block.tensor
            def _(pe):
                def outs(g):
                    pe.wait_ge(r_ready, g + 1)
                    if g >= 2:
                        pe.wait_ge(o_used, g - 1)
                    for j in range(GT):
                        for hf in range(2):
                            rr = slice(hf * S, hf * S + S)
                            tok = g * 512 + j * P + hf * S
                            last = pe.matmul(t.bank[4 + g % 2][rr, j * P:(j + 1) * P], qt[0:D, tok:tok + S], r[:, g % 2, hf * GT + j, :], start=True, stop=True)
                    last.then_inc(o_done, 1)
                for g in range(G):
                    if g >= 2:
                        pe.wait_ge(r_ready, g - 1)
                    for j in range(GT):
                        for hf in range(2):
                            rr = slice(hf * S, hf * S + S)
                            last = pe.matmul(t.bank[g % 2 * 2 + hf][0:D, j * (D + 1):(j + 1) * (D + 1)], k[rr, g * GT + j, :], va[rr, g * GT + j, :], start=True, stop=True)
                    last.then_inc(kv_done, 1)
                    if g >= 1:
                        outs(g - 1)
                outs(G - 1)

            @block.vector
            def _(v):
                c = Chain(v, own)
                mask = t.heads[:].unsqueeze(1).broadcast_to([D, GT, D])

                def divide(g):
                    v.wait_ge(o_done, g + 1)
                    o = t.bank[4 + g % 2][:, :].rearrange("p (j c) -> p j c", c=P)
                    dn = den[:, g % 2, :].rearrange("p (j c) -> p j c", c=D)
                    c.link(v.tensor_scalar(dn, o[:, :, D:2 * D], 1e-6, None, ALU.add))
                    c.link(v.reciprocal(dn, dn))
                    v.tensor_tensor(out[:, g * GT:(g + 1) * GT, :], o[:, :, 0:D], dn, ALU.mult).then_inc(o_used, 1)
                for g in range(G):
                    v.wait_ge(kv_done, g + 1)
                    if g >= 2:
                        v.wait_ge(o_done, g - 1)
                    for hf in range(2):
                        kv = t.bank[g % 2 * 2 + hf][0:D, 0:GT * (D + 1)].rearrange("p (j c) -> p j c", c=D + 1)
                        rh = r[:, g % 2, hf * GT:(hf + 1) * GT, :]
                        v.tensor_tensor(rh[:, :, 0:D], kv[:, :, 0:D], mask, ALU.mult)
                        last = v.tensor_tensor(rh[:, :, D:2 * D], kv[:, :, D:D + 1].broadcast_to([D, GT, D]), mask, ALU.mult)
                    last.then_inc(r_ready, 1)
                    if g >= 1:
                        divide(g - 1)
                divide(G - 1)


def act_dense_stage(t, xt, w, dst, func):
    with t.stage("m_done", "m_moved") as (block, m_done, m_moved):
        @block.tensor
        def _(pe):
            for g in range(G):
                if g >= 2:
                    pe.wait_ge(m_moved, g - 1)
                pe.matmul(t.bank[g % 2][0:D, :], w, xt[0:D + 1, g * 512:(g + 1) * 512], start=True, stop=True).then_inc(m_done, 1)

        @block.scalar
        def _(act):
            for g in range(G):
                act.wait_ge(m_done, g + 1)
                act.activation(dst[0:D, g * 512:(g + 1) * 512], t.bank[g % 2][0:D, :], func).then_inc(m_moved, 1)


def attention_buffers(t, ctx, name):
    x = t.sb(name + "_x", [P, IT, D], ctx=ctx)
    y = t.sb(name + "_y", [P, IT, D], ctx=ctx)
    z = t.sb(name + "_z", [P, IT, D], ctx=ctx)
    xt = t.sb(name + "_xt", [D + 1, IT * P], ctx=ctx)
    qt = t.sb(name + "_qt", [D + 1, IT * P], ctx=ctx)
    va = t.sb(name + "_va", [P, IT, D + 1], ctx=ctx)
    with t.stage("z") as (block, _z):
        @block.vector
        def _(v):
            v.memset(xt[D:D + 1, :], 1.0)
            v.memset(qt[D:D + 1, :], 1.0)
            v.memset(va[:, :, D:D + 1], 1.0)
    return x, y, z, xt, qt, va


def l2_attention(t, wq, wkv, g1, b1, w1, w2, g2, b2):
    nc = t.nc
    with ExitStack() as ctx:
        x, y, z, xt, qt, va = attention_buffers(t, ctx, "a2")
        with nc.Fori(0, STEPS) as it:
            h = t.h[:, bass.ds(it * IT, IT), :]
            norm_stage(t, h, x[:], 1e-5)
            turn_stage(t, x, xt)
            linear_attention(t, xt, wq, wkv, qt, y, va, z)
            add_stage(t, z[:], z[:], x[:])
            norm_stage(t, z[:], y[:], 1e-5, gain=g1, shift=b1)
            turn_stage(t, y, xt)
            act_dense_stage(t, xt, w1, qt, ACT.Gelu)
            dense_stage(t, qt, w2, z[:], D, base=y[:])
            norm_stage(t, z[:], x[:], 1e-5, gain=g2, shift=b2)
            add_stage(t, h, h, x[:])


def add_stage(t, out, a, b):
    with t.stage("z") as (block, z):
        @block.vector
        def _(v):
            v.tensor_tensor(out, a, b, ALU.add)


def l3_attention(t, n1, wq, wkv, wo, n2):
    nc = t.nc
    with ExitStack() as ctx:
        x, y, z, xt, qt, va = attention_buffers(t, ctx, "a3")
        with nc.Fori(0, STEPS) as it:
            h = t.h[:, bass.ds(it * IT, IT), :]
            norm_stage(t, h, x[:], 1e-5)
            norm_stage(t, x[:], y[:], 1e-6, centre=False, gain=n1)
            turn_stage(t, y, xt)
            linear_attention(t, xt, wq, wkv, qt, y, va, z)
            turn_stage(t, z, xt)
            dense_stage(t, xt, wo, z[:], D, base=x[:])
            norm_stage(t, z[:], x[:], 1e-6, centre=False, gain=n2, add_src=True)
            add_stage(t, h, h, x[:])


def l2_experts(t, gw, w1, w2, b2, gamma, beta):
    nc, E, F = t.nc, 8, 128
    cap = float(-(-5 * NB * S // (4 * E)))
    with ExitStack() as ctx:
        x = t.sb("e2_x", [P, IT, D], ctx=ctx)
        acc = t.sb("e2_acc", [P, IT, D], ctx=ctx)
        y = t.sb("e2_y", [P, IT, D], ctx=ctx)
        xt = t.sb("e2_xt", [D + 1, IT * P], ctx=ctx)
        gate_t = t.sb("e2_gt", [E, IT * P], ctx=ctx)
        mean = t.sb("e2_mean", [D + 1, STEPS, 2 * IT], ctx=ctx)
        lg = t.sb("e2_lg", [P, 1, E], ctx=ctx)
        rw = t.sb("e2_rw", [P, 1, E], ctx=ctx)
        spread = t.sb("e2_spread", [P, TILES, E], ctx=ctx)
        all_gates = t.sb("e2_gates", [P, TILES, E], ctx=ctx)
        gates = t.sb("e2_g", [P, IT, E], ctx=ctx)
        b = {k: t.sb("e2_" + k, [P, 1], ctx=ctx)[:] for k in ("k1", "k2", "one", "tot")}
        b |= {k: t.sb("e2_" + k, [P, 1, E], ctx=ctx)[:] for k in ("p1", "p2")}
        with t.stage("z") as (block, z):
            @block.vector
            def _(v):
                v.memset(xt[D:D + 1, :], 1.0)
                v.memset(mean[D:D + 1, :, :], 1.0)
        with nc.Fori(0, STEPS) as it:
            norm_stage(t, t.h[:, bass.ds(it * IT, IT), :], x[:], 1e-5)
            with t.stage("m_done") as (block, m_done):
                @block.tensor
                def _(pe):
                    for k in range(IT):
                        last = pe.matmul(t.bank[0][0:D, 2 * k:2 * k + 2], x[:, k, :], t.halves[:, :], start=True, stop=True)
                    last.then_inc(m_done, 1)

                @block.vector
                def _(v):
                    v.wait_ge(m_done, 1)
                    v.tensor_scalar(mean[0:D, bass.ds(it, 1), :].squeeze(1), t.bank[0][0:D, 0:2 * IT], 1.0 / S, None, ALU.mult)
        with t.stage("l_done", "l_moved") as (block, l_done, l_moved):
            @block.tensor
            def _(pe):
                pe.matmul(t.bank[0][:, 0:E], mean[:].rearrange("p a b -> p (a b)"), gw, start=True, stop=True).then_inc(l_done, 1)

            @block.vector
            def _(v):
                v.wait_ge(l_done, 1)
                v.tensor_copy(lg[:, 0, :], t.bank[0][:, 0:E]).then_inc(l_moved, 1)
        exp_rows(t, lg[:], b["k1"], b["tot"], 1, E)
        with t.stage("own", "p_ready", "load_done") as (block, own, p_ready, load_done):
            @block.vector
            def _(v):
                c = Chain(v, own)
                v.tensor_tensor(rw[:], lg[:], bc(b["tot"], E), ALU.mult).then_inc(p_ready, 1)
                v.wait_ge(load_done, 1)
                load = b["p1"][:, 0, :]
                over = b["p2"][:, 0, :]
                c.link(v.tensor_scalar(load, t.bank[0][:, 0:E], float(S), None, ALU.mult))
                c.link(v.tensor_scalar(over, load, cap, None, ALU.is_gt))
                c.link(v.reciprocal(load, load))
                c.link(v.tensor_scalar(load, load, cap, -1.0, ALU.mult, ALU.add))
                c.link(v.tensor_scalar(load, load, 0.0, None, ALU.min))
                c.link(v.tensor_tensor(load, load, over, ALU.mult))
                c.link(v.tensor_scalar(load, load, 1.0, None, ALU.add))
                c.link(v.tensor_tensor(lg[:, 0, :], rw[:, 0, :], load, ALU.mult))

            @block.tensor
            def _(pe):
                pe.wait_ge(p_ready, 1)
                pe.matmul(t.bank[0][:, 0:E], t.ones[:, :], rw[:, 0, :], start=True, stop=True).then_inc(load_done, 1)
        exp_rows(t, lg[:], b["k1"], b["tot"], 1, E)
        with t.stage("own", "w_ready", "exped", "spread_ready", "g_done") as (block, own, w_ready, exped, spread_ready, g_done):
            @block.vector
            def _(v):
                c = Chain(v, own)
                c.link(v.tensor_tensor(lg[:], lg[:], bc(b["tot"], E), ALU.mult))
                top_two(c, v, t, lg[:], None, b, rw[:])
                v.tensor_tensor(b["one"], b["k2"], b["k1"], ALU.subtract).then_inc(w_ready, 1)
                v.wait_ge(exped, 1)
                c.link(v.tensor_scalar(b["tot"], b["one"], 1.0, None, ALU.add))
                c.link(v.reciprocal(b["tot"], b["tot"]))
                c.link(v.tensor_tensor(b["p2"], b["p2"], bc(b["one"], E), ALU.mult))
                c.link(v.tensor_tensor(b["p1"], b["p1"], b["p2"], ALU.add))
                c.link(v.tensor_tensor(b["p1"], b["p1"], bc(b["tot"], E), ALU.mult))
                v.tensor_tensor(spread[:], t.own_tile[:, :].unsqueeze(2).broadcast_to([P, TILES, E]),
                                b["p1"].broadcast_to([P, TILES, E]), ALU.mult).then_inc(spread_ready, 1)
                v.wait_ge(g_done, 1)
                v.tensor_copy(all_gates[:].rearrange("p k e -> p (k e)"), t.bank[1][:, :])

            @block.scalar
            def _(act):
                act.wait_ge(w_ready, 1)
                act.activation(b["one"], b["one"], ACT.Exp).then_inc(exped, 1)

            @block.tensor
            def _(pe):
                pe.wait_ge(spread_ready, 1)
                pe.matmul(t.bank[1][:, :], t.own_half[:, :], spread[:].rearrange("p k e -> p (k e)"), start=True, stop=True).then_inc(g_done, 1)
        with nc.Fori(0, STEPS) as it:
            h = t.h[:, bass.ds(it * IT, IT), :]
            norm_stage(t, h, x[:], 1e-5)
            with t.stage("z") as (block, z):
                @block.vector
                def _(v):
                    v.tensor_copy(gates[:], all_gates[:, bass.ds(it * IT, IT), :])
            turn_stage(t, x, xt)
            experts(t, "e2", x, xt, gate_t, E, F, ACT.Gelu, w1, w2, b2, acc, gates, x)
            norm_stage(t, acc[:], y[:], 1e-5, gain=gamma, shift=beta)
            add_stage(t, h, h, y[:])


def l3_experts(t, scores, w1, w2, b2):
    nc, E, F = t.nc, 4, 128
    with ExitStack() as ctx:
        x = t.sb("e3_x", [P, IT, D], ctx=ctx)
        acc = t.sb("e3_acc", [P, IT, D], ctx=ctx)
        xt = t.sb("e3_xt", [D + 1, IT * P], ctx=ctx)
        gate_t = t.sb("e3_gt", [E, IT * P], ctx=ctx)
        lg = t.sb("e3_lg", [P, IT, E], ctx=ctx)
        gates = t.sb("e3_g", [P, IT, E], ctx=ctx)
        b = {k: t.sb("e3_" + k, [P, IT], ctx=ctx)[:] for k in ("k1", "k2", "one", "tot")}
        b |= {k: t.sb("e3_" + k, [P, IT, E], ctx=ctx)[:] for k in ("p1", "p2")}
        with t.stage("z") as (block, z):
            @block.vector
            def _(v):
                v.memset(xt[D:D + 1, :], 1.0)
        with nc.Fori(0, STEPS) as it:
            h = t.h[:, bass.ds(it * IT, IT), :]
            norm_stage(t, h, x[:], 1e-5)
            turn_stage(t, x, xt)
            with t.stage("own", "w_ready", "exped") as (block, own, w_ready, exped):
                @block.vector
                def _(v):
                    c = Chain(v, own)
                    c.link(v.tensor_copy(lg[:], scores[:, bass.ds(it * IT, IT), :]))
                    pick_first(c, v, t, lg[:], b["k1"], b["p1"], b["one"], E)
                    c.link(v.scalar_tensor_tensor(gates[:], b["p1"], -1e30, lg[:], ALU.mult, ALU.add))
                    pick_first(c, v, t, gates[:], b["k2"], b["p2"], b["one"], E)
                    v.tensor_tensor(b["one"], b["k2"], b["k1"], ALU.subtract).then_inc(w_ready, 1)
                    v.wait_ge(exped, 1)
                    c.link(v.tensor_scalar(b["tot"], b["one"], 1.0, None, ALU.add))
                    c.link(v.reciprocal(b["tot"], b["tot"]))
                    c.link(v.tensor_tensor(b["p2"], b["p2"], bc(b["one"], E), ALU.mult))
                    c.link(v.tensor_tensor(b["p1"], b["p1"], b["p2"], ALU.add))
                    c.link(v.tensor_tensor(gates[:], b["p1"], bc(b["tot"], E), ALU.mult))

                @block.scalar
                def _(act):
                    act.wait_ge(w_ready, 1)
                    act.activation(b["one"], b["one"], ACT.Exp).then_inc(exped, 1)
            experts(t, "e3", x, xt, gate_t, E, F, ACT.Gelu, w1, w2, b2, acc, gates, None)
            add_stage(t, h, h, acc[:])


def l1_attention(t, wq, wk, wvf, wvb, fan, beside):
    nc, NH, Q4, I16, RD = t.nc, 8, 4, 16, 3
    with ExitStack() as ctx:
        x = t.sb("a1_x", [P, GT, D], ctx=ctx)
        o = t.sb("a1_o", [P, GT, D], ctx=ctx)
        sg = t.sb("a1_sg", [P, GT, D], ctx=ctx)
        xt = t.sb("a1_xt", [D + 1, GT * P], ctx=ctx)
        qs = t.sb("a1_q", [P, GT, NH, S], ctx=ctx)
        ks = t.sb("a1_k", [P, GT, NH, S], ctx=ctx)
        vf = t.sb("a1_vf", [P, GT, 2, NH * D], ctx=ctx)
        vb = t.sb("a1_vb", [P, GT, 2, 4, D], ctx=ctx)
        diff = t.sb("a1_diff", [P, RD, Q4, NH * S], ctx=ctx)
        ex = t.sb("a1_ex", [P, 512], ctx=ctx)
        ln = t.sb("a1_ln", [P, 512], ctx=ctx)
        a = t.sb("a1_a", [P, NH, S], ctx=ctx)
        at = t.sb("a1_at", [P, 4, P], ctx=ctx)
        with t.stage("z") as (block, z):
            @block.vector
            def _(v):
                v.memset(xt[D:D + 1, :], 1.0)
        by_image = xt[:, :].rearrange("p (k m s) -> p m k s", m=2, s=S)
        xq = t.sb("a1_xq", [D + 1, GT, P], ctx=ctx)
        from_image = xt[:, :].rearrange("p (k m q i) -> p m k q i", m=2, q=Q4, i=I16)
        by_quarter = xq[:, :, :].rearrange("p k (q m i) -> p m k q i", m=2, q=Q4)
        with nc.Fori(0, TILES // GT) as it:
            h = t.h[:, bass.ds(it * GT, GT), :]
            norm_stage(t, h, x[:], 1e-5)
            turn_stage(t, x, xt)
            steps = [("q", n) for n in range(4)] + [("k", 0)] + [("f", n) for n in range(GT)] + [("b", n) for n in range(GT)]
            with t.stage("p_done", "p_used", "ordered") as (block, p_done, p_used, ordered):
                @block.tensor
                def _(pe):
                    for n, (kind, j) in enumerate(steps):
                        if n >= 4:
                            pe.wait_ge(p_used, n - 3)
                        b = t.bank[n % 4]
                        if kind == "q":
                            for e in range(2):
                                for m in range(2):
                                    last = pe.matmul(b[m * D:(m + 1) * D, e * 256:(e + 1) * 256], wq[:, (2 * j + e) * D:(2 * j + e + 1) * D], by_image[:, m], start=True, stop=True)
                        elif kind == "k":
                            for m in range(2):
                                last = pe.matmul(b[m * D:(m + 1) * D, 0:256], t.ident[0:D, 0:D], by_image[0:D, m], start=True, stop=True)
                        elif kind == "f":
                            pe.wait_ge(ordered, 1)
                            last = pe.matmul(b[:, :], xq[:, j, :], wvf, start=True, stop=True)
                        else:
                            for m in range(2):
                                for e in range(2):
                                    last = pe.matmul(b[e * D:(e + 1) * D, m * 256:(m + 1) * 256], xt[:, j * P + m * S:j * P + m * S + S], wvb[:, e * 256:(e + 1) * 256], start=True, stop=True)
                        last.then_inc(p_done, 1)

                @block.scalar
                def _(act):
                    for n, (kind, j) in enumerate(steps):
                        b = t.bank[n % 4]
                        if kind == "k":
                            act.wait_ge(p_used, n + 1)
                            continue
                        act.wait_ge(p_done, n + 1)
                        if kind == "q":
                            last = act.activation(qs[:, :, 2 * j:2 * j + 2, :], b[:, :].rearrange("p (e k s) -> p k e s", e=2, s=S), ACT.Copy)
                        elif kind == "f":
                            for m in range(2):
                                last = act.activation(vf[:, j, m, :], b[:, :], ACT.Copy, scale=t.of_image[:, m:m + 1])
                        else:
                            last = act.activation(vb[:, j].rearrange("p m c w -> p (m c w)"), b[:, :], ACT.Copy)
                        last.then_inc(p_used, 1)

                @block.vector
                def _(v):
                    for m in range(2):
                        last = v.tensor_copy(by_quarter[:, m], from_image[:, m])
                    last.then_inc(ordered, 1)
                    v.wait_ge(p_done, 5)
                    v.wait_ge(p_used, 4)
                    for e in range(NH):
                        last = v.tensor_scalar(ks[:, :, e, :], t.bank[4 % 4][:, 0:256].rearrange("p (k s) -> p k s", s=S), wk[:, e:e + 1], None, ALU.mult)
                    last.then_inc(p_used, 1)
            with t.stage("diff_done", "abs_done", "sum_done", "ex_done", "den_done", "ln_done", "t_done", "a_done", "at_done", "at_moved", "o_done", "o_moved", "f_loaded", "pool_sent") as \
                    (block, diff_done, abs_done, sum_done, ex_done, den_done, ln_done, t_done, a_done, at_done, at_moved, o_done, o_moved, loaded, scattered):
                @block.sync
                def _(sp):
                    beside.fetch(sp, it, loaded)
                    sp.wait_ge(loaded, 32)

                @block.gpsimd
                def _(p):
                    p.wait_ge(loaded, 32)
                    beside.send(p, scattered)

                EXP1, DEN, LN, ADD, EXP2, TURN, MOVE, OUT, TAKE = 0, 1, 2, 3, 4, 5, 6, 7, 8

                def each(eng, step, pieces):
                    for k in range(GT + 1):
                        for i in range(I16):
                            if k < GT:
                                step(k * I16 + i, k, i)
                            if k >= 1 and i in pieces:
                                pieces[i](k - 1)

                @block.vector
                def _(v):
                    def step(n, k, i):
                        if n >= RD:
                            v.wait_ge(sum_done, n - RD + 1)
                        q = qs[:, k, :, i:S:I16].rearrange("p h q -> p q h").unsqueeze(3).broadcast_to([P, Q4, NH, S])
                        kk = ks[:, k].unsqueeze(1).broadcast_to([P, Q4, NH, S])
                        v.tensor_tensor(diff[:, n % RD].rearrange("p q (h s) -> p q h s", s=S), q, kk, ALU.subtract).then_inc(diff_done, 1)

                    def add(k):
                        v.wait_ge(ln_done, k + 1)
                        v.scalar_tensor_tensor(ln[:], ln[:], 8.0, t.bank[k % 2][:, :], ALU.mult, ALU.add).then_inc(t_done, 1)

                    def take(k):
                        v.wait_ge(o_done, k + 1)
                        v.tensor_copy(o[:, k, :], t.bank[4][:, 0:D]).then_inc(o_moved, 1)
                    each(v, step, {ADD: add, TAKE: take})

                @block.scalar
                def _(act):
                    def step(n, k, i):
                        act.wait_ge(diff_done, n + 1)
                        d = diff[:, n % RD].rearrange("p q c -> p (q c)")
                        act.activation(d, d, ACT.Abs).then_inc(abs_done, 1)

                    def exp1(k):
                        act.wait_ge(sum_done, (k + 1) * I16)
                        act.activation(ex[:], t.bank[k % 2][:, :], ACT.Exp, scale=-0.125).then_inc(ex_done, 1)

                    def log(k):
                        act.wait_ge(den_done, k + 1)
                        act.activation(ln[:], t.bank[2][:, :], ACT.Ln, bias=1.0).then_inc(ln_done, 1)

                    def exp2(k):
                        act.wait_ge(t_done, k + 1)
                        if k >= 1:
                            act.wait_ge(o_done, k)
                        act.activation(a[:].rearrange("p h s -> p (h s)"), ln[:], ACT.Exp, scale=-0.125).then_inc(a_done, 1)

                    def move(k):
                        act.wait_ge(at_done, k + 1)
                        for m in range(2):
                            last = act.activation(at[:, :, m * S:(m + 1) * S].rearrange("p c (q i) -> p c q i", q=Q4),
                                                  t.bank[3][:, :].rearrange("p (c q m i) -> p m c q i", q=Q4, m=2, i=I16)[:, m], ACT.Copy)
                        last.then_inc(at_moved, 1)
                    each(act, step, {EXP1: exp1, LN: log, EXP2: exp2, MOVE: move})

                @block.tensor
                def _(pe):
                    def step(n, k, i):
                        pe.wait_ge(abs_done, n + 1)
                        if i == 0 and k >= 2:
                            pe.wait_ge(t_done, k - 1)
                        for q in range(Q4):
                            last = pe.matmul(t.bank[k % 2][32 * q:32 * q + 32, :], t.pick_row[:, i, :], diff[:, n % RD, q, :], start=(i == 0), stop=(i == I16 - 1))
                        last.then_inc(sum_done, 1)

                    def den(k):
                        pe.wait_ge(ex_done, k + 1)
                        if k >= 1:
                            pe.wait_ge(ln_done, k)
                        pe.matmul(t.bank[2][:, :], t.same_image[:, :], ex[:], start=True, stop=True).then_inc(den_done, 1)

                    def turn(k):
                        pe.wait_ge(a_done, k + 1)
                        for c in range(4):
                            last = pe.transpose(t.bank[3][:, c * P:(c + 1) * P], a[:, 2 * c:2 * c + 2, :].rearrange("p e s -> p (e s)"), t.ident[:, :])
                        last.then_inc(at_done, 1)

                    def out(k):
                        pe.wait_ge(at_moved, k + 1)
                        if k >= 1:
                            pe.wait_ge(o_moved, k)
                        for m in range(2):
                            dst = t.bank[4][m * S:(m + 1) * S, 0:D]
                            for e in range(NH):
                                pe.matmul(dst, a[:, e, :], vf[:, k, m, e * D:(e + 1) * D], start=(e == 0), stop=False)
                            for c in range(4):
                                last = pe.matmul(dst, at[:, c, m * S:(m + 1) * S], vb[:, k, m, c, :], start=False, stop=(c == 3))
                        last.then_inc(o_done, 1)
                    each(pe, step, {DEN: den, TURN: turn, OUT: out})
            with t.stage("sg_done", "y_ready") as (block, sg_done, y_ready):
                @block.scalar
                def _(act):
                    act.activation(sg[:], o[:], ACT.Sigmoid, scale=1.702).then_inc(sg_done, 1)

                @block.vector
                def _(v):
                    v.wait_ge(sg_done, 1)
                    v.tensor_tensor(o[:], o[:], sg[:], ALU.mult)
            turn_stage(t, o, xt)
            dense_stage(t, xt, fan, o[:], D, base=x[:])
            add_stage(t, h, h, o[:])


NODES = NB * S
EDGES = 262144
LISTED = EDGES + NODES
COLS = LISTED // P
RUN = 64
CHUNKS_E = LISTED // (P * RUN)
ROWS = LISTED // RUN
HD, EX = 4, 4
ST = HD * (EX + 2)
TB = HD * EX + 2 * HD


def clear_pool_dma(p, sem):
    p.dma_reset(range(sem.num, sem.num + 1))
    p.sem_clear(sem)


def rank_stage(t, b, key, bins, shift):
    nc = t.nc
    hist, base = b["hist"], b["base"]
    with t.stage("own", "counted", "summed") as (block, own, counted, summed):
        @block.vector
        def _(v):
            c = Chain(v, own)
            with v.Fori(0, bins) as i:
                v.sem_clear(own)
                c.n = 0
                c.link(v.tensor_scalar(b["hit"][:], key, t.iota[:, bass.ds(i, 1)], None, ALU.is_equal, ALU.add, accum_out=b["one"][:]))
                c.link(v.tensor_copy(hist[:, bass.ds(i, 1)], b["one"][:]))
            v.sem_clear(own)
            c.n = 0
            v.tensor_copy(base[:, 0:bins], hist[:, 0:bins]).then_inc(counted, 1)
            v.wait_ge(summed, 1)
            c.link(v.tensor_tensor_scan(base[:, 0:bins], t.bank[1][:, 0:bins], hist[:, 0:bins], float(shift - 1), ALU.add, ALU.bypass))
            c.link(v.tensor_copy(b["incl"][:, 0:bins], base[:, 0:bins]))
            c.link(v.tensor_tensor(base[:, 0:bins], base[:, 0:bins], t.bank[1][:, 0:bins], ALU.subtract))
            c.link(v.tensor_tensor(base[:, 0:bins], base[:, 0:bins], t.bank[0][:, 0:bins], ALU.add))
            with v.Fori(0, bins) as i:
                v.sem_clear(own)
                c.n = 0
                c.link(v.tensor_scalar(b["hit"][:], key, t.iota[:, bass.ds(i, 1)], None, ALU.is_equal))
                c.link(v.tensor_copy(b["one"][:], base[:, bass.ds(i, 1)]))
                c.link(v.tensor_tensor_scan(b["run"][:], b["hit"][:], b["hit"][:], b["one"][:, 0:1], ALU.add, ALU.bypass))
                c.link(v.copy_predicated(b["posf"][:], b["hit"][:].bitcast(mybir.dt.uint16), b["run"][:]))
            v.sem_clear(own)
            c.n = 0
            c.link(v.tensor_copy(b["pos"][:], b["posf"][:]))

        @block.tensor
        def _(pe):
            pe.wait_ge(counted, 1)
            pe.matmul(t.bank[0][:, 0:bins], t.before[:, :], hist[:, 0:bins], start=True, stop=True)
            pe.matmul(t.bank[1][:, 0:bins], t.ones[:, :], hist[:, 0:bins], start=True, stop=True).then_inc(summed, 1)


class Scatter:

    def __init__(self, t, ctx, name, n, place, edges, dst):
        self.n, self.place, self.edges, self.dst = n, place, edges, dst
        self.idx = t.sb(name + "_idx", [P, n], I32, ctx=ctx)
        self.rows = t.sb(name + "_rows", [P, n, 2], I32, ctx=ctx)

    def fetch(self, sp, step, loaded):
        sp.dma_start(self.idx[:], self.place[:, bass.ds(step * self.n, self.n)]).then_inc(loaded, 16)
        sp.dma_start(self.rows[:], self.edges[:, bass.ds(step * self.n, self.n), :]).then_inc(loaded, 16)

    def send(self, p, sent):
        for k in range(self.n):
            p.indirect_dma_start(out=self.dst, out_offset=bass.IndirectOffsetOnAxis(ap=self.idx[:, k:k + 1], axis=0),
                                 in_=self.rows[:, k, :], in_offset=None).then_inc(sent, 16)
        p.wait_ge(sent, 16 * self.n)


def rank_buffers(t, ctx):
    sb = lambda name, shape, dt=F32: t.sb("s_" + name, shape, dt, ctx=ctx)
    b = {k: sb(k, [P, COLS]) for k in ("mask", "run", "posf", "key")}
    b |= {k: sb(k, [P, COLS], BF16) for k in ("small_key", "hit")}
    b["pos"] = sb("pos", [P, COLS], I32)
    b |= {k: sb(k, [P, P]) for k in ("hist", "base", "incl")}
    b["one"] = sb("one", [P, 1])
    return b


def rank_by_column(t, d):
    with ExitStack() as ctx:
        sb = lambda name, shape, dt=F32: t.sb("s_" + name, shape, dt, ctx=ctx)
        edges = sb("edges", [P, COLS, 2], I32)
        b = rank_buffers(t, ctx)
        minus = sb("minus", [1, 2], I32)
        node, source, ints = b["key"], b["run"], b["pos"]
        with t.stage("f_loaded", "own") as (block, loaded, own):
            @block.sync
            def _(sp):
                sp.dma_start(edges[:], d["edges"]).then_inc(loaded, 16)
                sp.wait_ge(loaded, 16)

            @block.vector
            def _(v):
                c = Chain(v, own)
                v.wait_ge(loaded, 16)
                c.link(v.memset(b["posf"][:], 0.0))
                c.link(v.memset(minus[:], -1))
                c.link(v.tensor_copy(node[:], edges[:, :, 1]))
                c.link(v.tensor_scalar(b["mask"][:], node[:], 0.0, float(1 << 20), ALU.is_lt, ALU.mult))
                c.link(v.tensor_tensor(node[:], node[:], b["mask"][:], ALU.max))
                c.link(v.tensor_scalar(node[:], node[:], float(NODES), None, ALU.min))
                c.link(v.tensor_copy(edges[:, :, 1], node[:]))
                c.link(v.tensor_copy(source[:], edges[:, :, 0]))
                c.link(v.tensor_scalar(b["mask"][:], source[:], 0.0, float(NODES), ALU.is_lt, ALU.mult))
                c.link(v.tensor_tensor(source[:], source[:], b["mask"][:], ALU.add))
                c.link(v.tensor_scalar(source[:], source[:], float(NODES - 1), 0.0, ALU.min, ALU.max))
                c.link(v.tensor_copy(edges[:, :, 0], source[:]))
                c.link(v.tensor_scalar(ints[:], edges[:, :, 1], P - 1, None, ALU.bitwise_and))
                c.link(v.tensor_copy(b["small_key"][:], ints[:]))
        rank_stage(t, b, b["small_key"][:], P, 0)
        with t.stage("sent") as (block, sent):
            @block.sync
            def _(sp):
                sp.dma_start(d["listed"], edges[:]).then_inc(sent, 16)
                sp.dma_start(d["place1"].rearrange("(p c) -> p c", p=P), b["pos"][:]).then_inc(sent, 16)
                sp.dma_start(d["sorted2"][0:1, :], minus[:]).then_inc(sent, 16)
                sp.wait_ge(sent, 48)


def rank_by_row(t, d):
    bins = NODES // P + 1
    with ExitStack() as ctx:
        nodes = t.sb("s_nodes", [P, COLS, 2], I32, ctx=ctx)
        b = rank_buffers(t, ctx)
        ends = t.sb("s_ends", [P, 1], I32, ctx=ctx)
        with t.stage("f_loaded", "own") as (block, loaded, own):
            @block.sync
            def _(sp):
                sp.dma_start(nodes[:], d["sorted1"].rearrange("(p c) w -> p c w", p=P)).then_inc(loaded, 16)
                sp.wait_ge(loaded, 16)

            @block.vector
            def _(v):
                c = Chain(v, own)
                c.link(v.memset(b["posf"][:], 0.0))
                v.wait_ge(loaded, 16)
                c.link(v.tensor_scalar(b["pos"][:], nodes[:, :, 1], 7, None, ALU.logical_shift_right))
                c.link(v.tensor_copy(b["small_key"][:], b["pos"][:]))
        rank_stage(t, b, b["small_key"][:], bins, 1)
        with t.stage("own", "sent") as (block, own, sent):
            @block.vector
            def _(v):
                v.tensor_scalar(ends[:], b["incl"][:, bins - 2:bins - 1], 1.0, None, ALU.add).then_inc(own, 1)

            @block.sync
            def _(sp):
                sp.dma_start(d["place2"].rearrange("(p c) w -> p (c w)", p=P), b["pos"][:]).then_inc(sent, 16)
                sp.wait_ge(own, 1)
                sp.dma_start(d["starts"][NODES:NODES + 1].rearrange("(a b) -> a b", b=1), ends[0:1, :]).then_inc(sent, 16)
                sp.wait_ge(sent, 32)


def find_starts(t, d, start):
    with ExitStack() as ctx:
        where = t.sb("s_where", [P, TILES], I32, ctx=ctx)
        with t.stage("pool_sent", "f_loaded", "sent") as (block, gathered, loaded, sent):
            @block.gpsimd
            def _(p):
                p.wait_ge(loaded, 16)
                for k in range(TILES):
                    p.indirect_dma_start(out=start[:, 0, k:k + 1], out_offset=None, in_=d["place2"],
                                         in_offset=bass.IndirectOffsetOnAxis(ap=where[:, k:k + 1], axis=0)).then_inc(gathered, 16)
                p.wait_ge(gathered, 16 * TILES)

            @block.sync
            def _(sp):
                sp.dma_start(where[:], d["place1"][0:NODES].rearrange("(k p) -> p k", p=P), allow_slow_non_contiguous=True).then_inc(loaded, 16)
                sp.wait_ge(gathered, 16 * TILES)
                sp.dma_start(d["starts"][0:NODES].rearrange("(k p) -> p k", p=P), start[:, 0, :], allow_slow_non_contiguous=True).then_inc(sent, 16)
                sp.wait_ge(sent, 16)
                sp.dma_start(start[:, 1, :], d["starts"][1:NODES + 1].rearrange("(k p) -> p k", p=P), allow_slow_non_contiguous=True).then_inc(sent, 16)
                sp.wait_ge(sent, 32)


def graph_attention(t, d, start, wg, att_src, att_dst, b_gat, gamma, beta, scores):
    nc = t.nc
    NEG = -1e30
    with ExitStack() as outer:
        tails = t.sb("g_tails", [P, CHUNKS_E, 3, 20], ctx=outer)
        with ExitStack() as ctx:
            sb = lambda name, shape, dt=F32: t.sb("g_" + name, shape, dt, ctx=ctx)
            tab_w = sb("tab_w", [D, TB])
            prod = sb("prod", [D, HD * EX])
            x = sb("x", [P, IT, D])
            xt = sb("xt", [D + 1, IT * P])
            tab = sb("tab", [P, IT, TB])
            with t.stage("own") as (block, own):
                @block.vector
                def _(v):
                    c = Chain(v, own)
                    c.link(v.tensor_copy(tab_w[:, 0:16], wg))
                    for n, a in enumerate((att_src, att_dst)):
                        c.link(v.tensor_tensor(prod[:], wg, a, ALU.mult))
                        c.link(v.tensor_reduce(tab_w[:, 16 + HD * n:16 + HD * (n + 1)], prod[:].rearrange("p (h e) -> p h e", e=EX), AX, ALU.add))
            with nc.Fori(0, STEPS) as it:
                norm_stage(t, t.h[:, bass.ds(it * IT, IT), :], x[:], 1e-5)
                turn_stage(t, x, xt)
                dense_stage(t, xt, tab_w[:], tab[:], TB, K=D)
                with t.stage("sent") as (block, sent):
                    @block.sync
                    def _(sp):
                        sp.dma_start(d["table"].rearrange("(i k p) f -> i p k f", p=P, k=IT)[bass.ds(it, 1)].squeeze(0), tab[:]).then_inc(sent, 16)
                        sp.wait_ge(sent, 16)
            es = sb("es", [P, 2, RUN, 2], I32)
            ep = sb("ep", [P, 2, RUN, 2], I32)
            first = sb("first", [P, 2], I32)
            idx = sb("idx", [P, 2, RUN], I32)
            flag = sb("flag", [P, RUN])
            keep = sb("keep", [P, RUN])
            nodef = sb("nodef", [P, 2, 2, RUN])
            begin = sb("begin", [P, 1])
            g = sb("g", [P, 2, RUN, TB])
            g0 = sb("g0", [P, 2, TB])
            e = sb("e", [P, HD, RUN])
            a = sb("a", [P, HD, RUN])
            m = sb("m", [P, HD, RUN + 1])
            r = sb("r", [P, HD, RUN])
            vals = sb("vals", [P, HD, EX, RUN])
            st = sb("st", [P, RUN, HD, EX + 2])
            fence = sb("fence", [P, RUN])
            starts_here = sb("starts_here", [P, 1])
            tail3 = sb("tail3", [P, 3, 20])
            flat2 = d["sorted2"]
            def chunk(fetched, now):
                with t.stage("f_loaded", "own", "staged", "pool_gathered", "em", "ee_ready", "st_ready", "sent") as (block, loaded, own, staged, gathered, em, ee_ready, st_ready, sent):
                    if fetched is not None:
                        c_in, k_in = fetched

                        @block.gpsimd
                        def _(p):
                            p.wait_ge(staged, 1)
                            p.indirect_dma_start(out=g0[:, k_in, :], out_offset=None, in_=d["table"], in_offset=bass.IndirectOffsetOnAxis(ap=first[:, k_in:k_in + 1], axis=0)).then_inc(gathered, 16)
                            for j in range(RUN):
                                p.indirect_dma_start(out=g[:, k_in, j, :], out_offset=None, in_=d["table"], in_offset=bass.IndirectOffsetOnAxis(ap=idx[:, k_in, j:j + 1], axis=0)).then_inc(gathered, 16)
                            p.wait_ge(gathered, 16 * (RUN + 1))

                    @block.sync
                    def _(sp):
                        if fetched is not None:
                            for dst, off in ((es, 1), (ep, 0)):
                                src = flat2[off:off + LISTED, :].rearrange("(c p j) w -> c p j w", p=P, j=RUN)[bass.ds(c_in, 1)].squeeze(0)
                                sp.dma_start(dst[:, k_in], src).then_inc(loaded, 16)
                            sp.wait_ge(loaded, 32)
                        if now is not None:
                            sp.wait_ge(st_ready, 1)
                            sp.dma_start(d["states"].rearrange("(c p j) f -> c p (j f)", p=P, j=RUN)[bass.ds(now[0], 1)].squeeze(0), st[:].rearrange("p j h f -> p (j h f)")).then_inc(sent, 16)
                            sp.wait_ge(sent, 16)

                    @block.vector
                    def _(v):
                        c = Chain(v, own)
                        if fetched is not None:
                            v.wait_ge(loaded, 32)
                            v.tensor_copy(nodef[:, k_in, 0, :], es[:, k_in, :, 1])
                            v.tensor_copy(nodef[:, k_in, 1, :], ep[:, k_in, :, 1])
                            c.link(v.tensor_copy(idx[:, k_in], es[:, k_in, :, 0]))
                            c.link(v.tensor_scalar(begin[:], nodef[:, k_in, 0, 0:1], float(NODES - 1), None, ALU.min))
                            v.tensor_copy(first[:, k_in:k_in + 1], begin[:]).then_inc(staged, 1)
                        if now is None:
                            return
                        c_now, k = now
                        gn = g[:, k]
                        c.link(v.tensor_tensor(keep[:], nodef[:, k, 0, :], nodef[:, k, 1, :], ALU.is_equal))
                        c.link(v.tensor_scalar(flag[:], keep[:], -1.0, 1.0, ALU.mult, ALU.add))
                        for h in range(HD):
                            last = v.tensor_tensor(a[:, h, :], gn[:, :, 20 + h], flag[:], ALU.mult)
                        c.link(last)
                        for h in range(HD):
                            last = v.tensor_tensor_scan(e[:, h, :], keep[:], a[:, h, :], g0[:, k, 20 + h:21 + h], ALU.mult, ALU.add)
                        c.link(last)
                        c.link(v.tensor_tensor(e[:], e[:], gn[:, :, 16:20].rearrange("p j h -> p h j"), ALU.add))
                        c.link(v.scalar_tensor_tensor(e[:], e[:], 0.2, e[:], ALU.mult, ALU.max))
                        c.link(v.tensor_scalar(fence[:], flag[:], NEG, None, ALU.mult))
                        for h in range(HD):
                            last = v.tensor_tensor_scan(m[:, h, 1:RUN + 1], fence[:], e[:, h, :], NEG, ALU.add, ALU.max)
                        c.link(last)
                        c.link(v.tensor_copy(m[:, :, 0:1], m[:, :, 1:2]))
                        kept = keep[:].unsqueeze(1).broadcast_to([P, HD, RUN])
                        c.link(v.tensor_tensor(r[:], m[:, :, 0:RUN], m[:, :, 1:RUN + 1], ALU.subtract))
                        c.link(v.tensor_tensor(r[:], r[:], kept, ALU.mult))
                        v.tensor_tensor(e[:], e[:], m[:, :, 1:RUN + 1], ALU.subtract).then_inc(em, 1)
                        v.wait_ge(ee_ready, 2)
                        c.link(v.tensor_tensor(r[:], r[:], kept, ALU.mult))
                        for h in range(HD):
                            last = v.tensor_tensor(vals[:, h], gn[:, :, h * EX:(h + 1) * EX].rearrange("p j f -> p f j"),
                                                   e[:, h, :].unsqueeze(1).broadcast_to([P, EX, RUN]), ALU.mult)
                        c.link(last)
                        for h in range(HD):
                            for f in range(EX):
                                v.tensor_tensor_scan(st[:, :, h, f], r[:, h, :], vals[:, h, f, :], 0.0, ALU.mult, ALU.add)
                            last = v.tensor_tensor_scan(st[:, :, h, EX], r[:, h, :], e[:, h, :], 0.0, ALU.mult, ALU.add)
                        c.link(last)
                        c.link(v.tensor_copy(st[:, :, :, EX + 1], m[:, :, 1:RUN + 1].rearrange("p h j -> p j h")))
                        v.sem_inc(st_ready, 1)
                        t3 = tail3[:].rearrange("p a (h f) -> p a h f", f=EX + 1)
                        v.tensor_copy(t3[:, 0], st[:, RUN - 1, :, 0:EX + 1])
                        v.tensor_copy(t3[:, 1], st[:, RUN - 1, :, EX + 1:EX + 2].broadcast_to([P, HD, EX + 1]))
                        c.link(v.tensor_reduce(starts_here[:], flag[:], AX, ALU.max))
                        c.link(v.tensor_copy(tail3[:, 2, :], starts_here[:].broadcast_to([P, 20])))
                        c.link(v.tensor_copy(tails[:, bass.ds(c_now, 1)].squeeze(1), tail3[:]))

                    if now is not None:
                        @block.scalar
                        def _(act):
                            act.wait_ge(em, 1)
                            act.activation(r[:], r[:], ACT.Exp).then_inc(ee_ready, 1)
                            act.activation(e[:], e[:], ACT.Exp).then_inc(ee_ready, 1)

            chunk((0, 0), None)
            with nc.Fori(0, CHUNKS_E // 2) as i:
                chunk((i * 2 + 1, 1), (i * 2, 0))
                chunk((i * 2 + 2, 0), (i * 2 + 1, 1))
            chunk(None, (CHUNKS_E - 1, 0))
        with ExitStack() as ctx:
            sb = lambda name, shape, dt=F32: t.sb("h_" + name, shape, dt, ctx=ctx)
            line = sb("line", [20, 3, ROWS])
            mm = sb("mm", [20, ROWS + 1])
            ww = sb("ww", [20, ROWS])
            carry = sb("carry", [P, CHUNKS_E, 2, 20])
            co = sb("co", [P, CHUNKS_E, HD, EX + 2])
            back = sb("back", [20, 2, ROWS])
            with t.stage("turned", "moved") as (block, turned, moved):
                @block.tensor
                def _(pe):
                    for n in range(CHUNKS_E):
                        if n >= 2:
                            pe.wait_ge(moved, n - 1)
                        for k in range(3):
                            last = pe.transpose(t.bank[n % 2][0:20, k * P:(k + 1) * P], tails[:, n, k, :], t.ident[:, :])
                        last.then_inc(turned, 1)

                @block.vector
                def _(v):
                    for n in range(CHUNKS_E):
                        v.wait_ge(turned, n + 1)
                        v.tensor_copy(line[:, :, n * P:(n + 1) * P], t.bank[n % 2][0:20, 0:3 * P].rearrange("p (k r) -> p k r", r=P)).then_inc(moved, 1)
            with t.stage("own", "diffs", "exped") as (block, own, diffs, exped):
                @block.vector
                def _(v):
                    c = Chain(v, own)
                    c.link(v.tensor_scalar(ww[:], line[:, 2, :], NEG, None, ALU.mult))
                    c.link(v.tensor_tensor_scan(mm[:, 1:ROWS + 1], ww[:], line[:, 1, :], NEG, ALU.add, ALU.max))
                    c.link(v.tensor_copy(mm[:, 0:1], mm[:, 1:2]))
                    c.link(v.tensor_scalar(line[:, 2, :], line[:, 2, :], -1.0, 1.0, ALU.mult, ALU.add))
                    c.link(v.tensor_tensor(ww[:], mm[:, 0:ROWS], mm[:, 1:ROWS + 1], ALU.subtract))
                    c.link(v.tensor_tensor(ww[:], ww[:], line[:, 2, :], ALU.mult))
                    v.tensor_tensor(line[:, 1, :], line[:, 1, :], mm[:, 1:ROWS + 1], ALU.subtract).then_inc(diffs, 1)
                    v.wait_ge(exped, 2)
                    c.link(v.tensor_tensor(ww[:], ww[:], line[:, 2, :], ALU.mult))
                    c.link(v.tensor_tensor(line[:, 0, :], line[:, 0, :], line[:, 1, :], ALU.mult))
                    c.link(v.tensor_tensor_scan(back[:, 0, :], ww[:], line[:, 0, :], 0.0, ALU.mult, ALU.add))
                    c.link(v.tensor_copy(back[:, 1, :], mm[:, 1:ROWS + 1]))

                @block.scalar
                def _(act):
                    act.wait_ge(diffs, 1)
                    act.activation(ww[:], ww[:], ACT.Exp).then_inc(exped, 1)
                    act.activation(line[:, 1, :], line[:, 1, :], ACT.Exp).then_inc(exped, 1)
            with t.stage("turned", "moved", "own", "sent") as (block, turned, moved, own, sent):
                @block.tensor
                def _(pe):
                    for n in range(CHUNKS_E):
                        if n >= 2:
                            pe.wait_ge(moved, n - 1)
                        for k in range(2):
                            last = pe.transpose(t.bank[n % 2][:, k * 20:(k + 1) * 20], back[:, k, n * P:(n + 1) * P], t.ident[0:20, 0:20])
                        last.then_inc(turned, 1)

                @block.vector
                def _(v):
                    c = Chain(v, own)
                    for n in range(CHUNKS_E):
                        v.wait_ge(turned, n + 1)
                        v.tensor_copy(carry[:, n].rearrange("p k f -> p (k f)"), t.bank[n % 2][:, 0:40]).then_inc(moved, 1)
                    v.wait_ge(moved, CHUNKS_E)
                    for n in range(CHUNKS_E):
                        v.tensor_copy(co[:, n, :, 0:EX + 1], carry[:, n, 0].rearrange("p (h f) -> p h f", f=EX + 1))
                        last = v.tensor_copy(co[:, n, :, EX + 1:EX + 2], carry[:, n, 1].rearrange("p (h f) -> p h f", f=EX + 1)[:, :, 0:1])
                    c.link(last)
                    c.link(v.memset(ww[0:1, 0:ST], 0.0))

                @block.sync
                def _(sp):
                    sp.wait_ge(own, 2)
                    dst = d["carries"][1:ROWS + 1, :].rearrange("(c p) f -> p c f", p=P)
                    sp.dma_start(dst, co[:].rearrange("p c h f -> p c (h f)")).then_inc(sent, 16)
                    sp.dma_start(d["carries"][0:1, :], ww[0:1, 0:ST]).then_inc(sent, 16)
                    sp.wait_ge(sent, 32)
        with ExitStack() as ctx:
            sb = lambda name, shape, dt=F32: t.sb("k_" + name, shape, dt, ctx=ctx)
            end = sb("end", [P, TILES], I32)
            row = sb("row", [P, 2, TILES], I32)
            rowf = sb("rowf", [P, 3, TILES])
            se = sb("se", [P, TILES, HD, EX + 2])
            sc = sb("sc", [P, TILES, HD, EX + 2])
            mx = sb("mx", [P, TILES, HD])
            wa = sb("wa", [P, TILES, HD])
            wb = sb("wb", [P, TILES, HD])
            agg = sb("agg", [P, TILES, HD, EX])
            tmp = sb("tmp", [P, TILES, HD, EX])
            s1 = sb("s1", [P, TILES])
            s2 = sb("s2", [P, TILES])
            with t.stage("own", "staged", "pool_gathered", "diffs", "exped", "var_ready", "std_ready") as (block, own, staged, gathered, diffs, exped, var_ready, std_ready):
                @block.gpsimd
                def _(p):
                    p.wait_ge(staged, 1)
                    for k in range(TILES):
                        p.indirect_dma_start(out=se[:, k].rearrange("p h f -> p (h f)"), out_offset=None, in_=d["states"], in_offset=bass.IndirectOffsetOnAxis(ap=end[:, k:k + 1], axis=0)).then_inc(gathered, 16)
                        p.indirect_dma_start(out=sc[:, k].rearrange("p h f -> p (h f)"), out_offset=None, in_=d["carries"], in_offset=bass.IndirectOffsetOnAxis(ap=row[:, 1, k:k + 1], axis=0)).then_inc(gathered, 16)
                    p.wait_ge(gathered, 32 * TILES)

                @block.scalar
                def _(act):
                    act.wait_ge(diffs, 1)
                    act.activation(wa[:], wa[:], ACT.Exp).then_inc(exped, 1)
                    act.activation(wb[:], wb[:], ACT.Exp).then_inc(exped, 1)
                    act.wait_ge(var_ready, 1)
                    act.activation(s2[:], s2[:], ACT.Sqrt).then_inc(std_ready, 1)

                @block.vector
                def _(v):
                    c = Chain(v, own)
                    c.link(v.tensor_copy(rowf[:, 0:2, :], start[:]))
                    c.link(v.tensor_scalar(rowf[:, 0, :], rowf[:, 0, :], -1.0, None, ALU.add))
                    c.link(v.tensor_scalar(rowf[:, 1, :], rowf[:, 1, :], -2.0, None, ALU.add))
                    c.link(v.tensor_copy(row[:], rowf[:, 0:2, :]))
                    c.link(v.tensor_copy(end[:], rowf[:, 1, :]))
                    c.link(v.tensor_scalar(row[:], row[:], 6, None, ALU.logical_shift_right))
                    v.tensor_copy(rowf[:, 0:2, :], row[:]).then_inc(staged, 1)
                    v.wait_ge(staged, 1)
                    c.link(v.tensor_tensor(rowf[:, 2, :], rowf[:, 0, :], rowf[:, 1, :], ALU.is_lt))
                    c.link(v.tensor_scalar(rowf[:, 1, :], rowf[:, 2, :], -1.0, -NEG, ALU.add, ALU.mult))
                    v.wait_ge(gathered, 32 * TILES)
                    used = rowf[:, 2, :].unsqueeze(2).broadcast_to([P, TILES, HD])
                    c.link(v.tensor_tensor(wb[:], sc[:, :, :, EX + 1], used, ALU.mult))
                    c.link(v.tensor_tensor(wb[:], wb[:], rowf[:, 1, :].unsqueeze(2).broadcast_to([P, TILES, HD]), ALU.add))
                    c.link(v.tensor_tensor(mx[:], wb[:], se[:, :, :, EX + 1], ALU.max))
                    c.link(v.tensor_tensor(wb[:], wb[:], mx[:], ALU.subtract))
                    v.tensor_tensor(wa[:], se[:, :, :, EX + 1], mx[:], ALU.subtract).then_inc(diffs, 1)
                    v.wait_ge(exped, 2)
                    for h in range(HD):
                        v.tensor_tensor(se[:, :, h, 0:EX + 1], se[:, :, h, 0:EX + 1], bc(wa[:, :, h], EX + 1), ALU.mult)
                        last = v.tensor_tensor(sc[:, :, h, 0:EX + 1], sc[:, :, h, 0:EX + 1], bc(wb[:, :, h], EX + 1), ALU.mult)
                    c.link(last)
                    c.link(v.tensor_tensor(se[:, :, :, 0:EX + 1].rearrange("p k h f -> p (k h) f"), se[:, :, :, 0:EX + 1].rearrange("p k h f -> p (k h) f"), sc[:, :, :, 0:EX + 1].rearrange("p k h f -> p (k h) f"), ALU.add))
                    c.link(v.tensor_scalar(wa[:], se[:, :, :, EX], 1e-16, None, ALU.add))
                    c.link(v.reciprocal(wa[:], wa[:]))
                    for h in range(HD):
                        last = v.tensor_tensor(agg[:, :, h, :], se[:, :, h, 0:EX], bc(wa[:, :, h], EX), ALU.mult)
                    c.link(last)
                    af = agg[:].rearrange("p k h f -> p k (h f)")
                    tf = tmp[:].rearrange("p k h f -> p k (h f)")
                    wide = lambda q: q.unsqueeze(1).broadcast_to([P, TILES, HD * EX])
                    c.link(v.tensor_tensor(af, af, wide(b_gat), ALU.add))
                    c.link(v.tensor_reduce(s1[:], af, AX, ALU.add))
                    c.link(v.tensor_scalar(s1[:], s1[:], -1.0 / 16, None, ALU.mult))
                    c.link(v.tensor_tensor(af, af, bc(s1[:], 16), ALU.add))
                    c.link(v.tensor_tensor(tf, af, af, ALU.mult))
                    c.link(v.tensor_reduce(s2[:], tf, AX, ALU.add))
                    v.tensor_scalar(s2[:], s2[:], 1.0 / 16, 1e-5, ALU.mult, ALU.add).then_inc(var_ready, 1)
                    v.wait_ge(std_ready, 1)
                    c.link(v.reciprocal(s2[:], s2[:]))
                    c.link(v.tensor_tensor(af, af, bc(s2[:], 16), ALU.mult))
                    c.link(v.tensor_tensor(af, af, wide(gamma), ALU.mult))
                    c.link(v.tensor_tensor(af, af, wide(beta), ALU.add))
                    c.link(v.tensor_reduce(scores[:], agg[:].rearrange("p k h e -> p k e h"), AX, ALU.add))
                    c.link(v.tensor_scalar(scores[:], scores[:], 1.0 / HD, None, ALU.mult))

def shape_constants():
    f32 = np.float32
    row = np.arange(P)
    c = {}
    c["ident"] = np.eye(P)
    c["ones"] = np.ones((P, P))
    c["upto"] = np.triu(np.ones((P, P)))
    c["before"] = np.triu(np.ones((P, P)), 1)
    c["iota"] = np.tile(row, (P, 1))
    c["falling"] = np.tile(np.arange(8, 0, -1), (P, 1))
    c["heads"] = np.kron(np.eye(8), np.ones((8, 8)))
    c["halves"] = np.kron(np.eye(2), np.ones((64, 1)))
    c["own_tile"] = row[:, None] // 2 == np.arange(TILES)
    c["own_half"] = row[:, None] % 2 == row // S
    image, query, from_image = (row // 16) % 2, row % 16, row // 64
    c["of_image"] = image[:, None] == np.arange(2)
    c["same_image"] = image[:, None] == image
    col = np.arange(32)
    c["pick_row"] = (from_image[:, None, None] == (col // 16)[None, None]) & (np.arange(16)[None, :, None] == (col % 16)[None, None])
    return {k: np.ascontiguousarray(v.astype(f32)) for k, v in c.items()}


def rows(v):
    return np.tile(v[None], (P, 1))


def with_bias(w, b):
    return np.concatenate([w, b[None]], 0)


def experts_in(w1, b1):
    E, _, F = w1.shape
    return with_bias(w1.transpose(1, 0, 2).reshape(D, E * F), b1.reshape(E * F))


def experts_out(w2):
    E, F, _ = w2.shape
    return w2.reshape(E * F // P, P, D).transpose(1, 0, 2)


def tower_layout(inp):
    w = {}
    w["a0_q"] = inp["L0_attn_q_weight"]
    for key, pre, gate in (("e0", "L0_ffn_", None), ("e1", "L1_ffn_", None)):
        w[key + "_w1"] = experts_in(inp[pre + "w1"], inp[pre + "b1"])
        w[key + "_w2"] = experts_out(inp[pre + "w2"])
        w[key + "_b2"] = inp[pre + "b2"]
    for key, pre in (("e2", "L2_ffn_"), ("e3", "L3_ffn_")):
        w[key + "_w1"] = experts_in(inp[pre + "W1"], inp[pre + "b1"])
        w[key + "_w2"] = experts_out(inp[pre + "W2"])
        w[key + "_b2"] = inp[pre + "b2"]
    w["e0_gate"] = with_bias(inp["L0_ffn_gate_w"], inp["L0_ffn_gate_b"])
    w["e1_gate"] = inp["L1_ffn_router_w"].T
    w["e2_gate"] = with_bias(inp["L2_ffn_Wr"], inp["L2_ffn_br"])
    w["e2_gamma"], w["e2_beta"] = rows(inp["L2_ffn_gamma"]), rows(inp["L2_ffn_beta"])
    qv = with_bias(inp["L1_attn_wqv_w"].T, inp["L1_attn_wqv_b"])
    w["a1_q"], w["a1_vf"] = qv[:, 0:512], qv[:, 512:1024]
    w["a1_vb"] = qv[:, 1024:].reshape(D + 1, 4, 2, D).transpose(0, 2, 1, 3).reshape(D + 1, 512)
    w["a1_k"] = np.tile(inp["L1_attn_wk"].T, (2, 1))
    w["a1_out"] = with_bias(inp["L1_attn_fanin_w"].T, inp["L1_attn_fanin_b"])
    qkv = inp["L2_attn_Wqkv"].T
    w["a2_q"], w["a2_kv"] = qkv[:, 0:D], qkv[:, D:]
    w["a2_w1"] = with_bias(inp["L2_attn_W1"].T, inp["L2_attn_b1"])
    w["a2_w2"] = with_bias(inp["L2_attn_W2"].T, inp["L2_attn_b2"])
    for k in ("ln1_g", "ln1_b", "ln2_g", "ln2_b"):
        w["a2_" + k] = rows(inp["L2_attn_" + k])
    qkv = inp["L3_attn_w_qkv"]
    w["a3_q"], w["a3_kv"] = qkv[:, 0:D], qkv[:, D:]
    w["a3_out"] = with_bias(inp["L3_attn_w_out"], inp["L3_attn_b_out"])
    w["a3_norm1"], w["a3_norm2"] = rows(inp["L3_attn_w_norm1"]), rows(inp["L3_attn_w_norm2"])
    w["gat_w"] = inp["L3_ffn_W_gat"]
    w["gat_src"] = np.tile(inp["L3_ffn_att_src"].reshape(1, 16), (D, 1))
    w["gat_dst"] = np.tile(inp["L3_ffn_att_dst"].reshape(1, 16), (D, 1))
    for k in ("b_gat", "ln_gamma", "ln_beta"):
        w["gat_" + k] = rows(inp["L3_ffn_" + k])
    return {k: np.ascontiguousarray(v) for k, v in w.items()}


def edge_layout(edge_index):
    loops = np.arange(NODES, dtype=edge_index.dtype)
    listed = np.concatenate([np.stack([loops, loops]), edge_index], 1)
    return np.ascontiguousarray(listed.T).reshape(P, COLS, 2)


def load_stage(t, pairs):
    with t.stage("f_loaded") as (block, loaded):
        @block.sync
        def _(sp):
            for dst, src in pairs:
                sp.dma_start(dst[:], src).then_inc(loaded, 16)
            sp.wait_ge(loaded, 16 * len(pairs))


def vit_tower(nc, const, fno_in, weights, edges, out):
    with ExitStack() as ctx:
        t = Tower(nc, ctx)
        t.h = t.sb("h", [P, TILES, D])
        for k, a in const.items():
            t.const[k] = t.sb("sc_" + k, a.shape)
        load_stage(t, [(t.const[k], a) for k, a in const.items()])
        t.name_constants()
        d = {"edges": edges}
        for name, shape, dt in (("listed", [P, COLS, 2], I32), ("sorted1", [LISTED, 2], I32), ("sorted2", [LISTED + 1, 2], I32),
                                ("place1", [LISTED], I32), ("place2", [LISTED, 1], I32), ("starts", [NODES + 1], I32),
                                ("table", [NODES, TB], F32), ("states", [LISTED, ST], F32), ("carries", [ROWS + 1, ST], F32)):
            d[name] = nc.dram_tensor(name, shape, dt, kind="Internal").ap()
        rank_by_column(t, d)
        with ExitStack() as side:
            steps = IGROUPS * LAYERS * CHUNKS
            fno(t, fno_in, Scatter(t, side, "by_column", COLS // steps, d["place1"].rearrange("(p c) -> p c", p=P), d["listed"], d["sorted1"]))
        rank_by_row(t, d)
        t.n_mean = t.sb("n_mean", [P, IT])
        t.n_var = t.sb("n_var", [P, IT])
        t.n_tmp = t.sb("n_tmp", [P, IT, D])
        w = {k: t.sb("sw_" + k, a.shape) for k, a in weights.items()}
        start = t.sb("start", [P, 2, TILES], I32)
        scores = t.sb("scores", [P, TILES, 4])
        load_stage(t, [(w[k], a) for k, a in weights.items()])
        l0_attention(t, w["a0_q"][:])
        l0_experts(t, w["e0_gate"][:], w["e0_w1"], w["e0_w2"], w["e0_b2"])
        with ExitStack() as side:
            by_row = Scatter(t, side, "by_row", COLS // (TILES // GT), d["place2"].rearrange("(p c) w -> p (c w)", p=P),
                             d["sorted1"].rearrange("(p c) w -> p c w", p=P), d["sorted2"])
            l1_attention(t, w["a1_q"][:], w["a1_k"][:], w["a1_vf"][:], w["a1_vb"][:], w["a1_out"][:], by_row)
        find_starts(t, d, start)
        l1_experts(t, w["e1_gate"][:], w["e1_w1"], w["e1_w2"], w["e1_b2"])
        l2_attention(t, w["a2_q"][:], w["a2_kv"][:], w["a2_ln1_g"][:], w["a2_ln1_b"][:], w["a2_w1"][:], w["a2_w2"][:], w["a2_ln2_g"][:], w["a2_ln2_b"][:])
        l2_experts(t, w["e2_gate"][:], w["e2_w1"], w["e2_w2"], w["e2_b2"], w["e2_gamma"][:], w["e2_beta"][:])
        l3_attention(t, w["a3_norm1"][:], w["a3_q"][:], w["a3_kv"][:], w["a3_out"][:], w["a3_norm2"][:])
        graph_attention(t, d, start, w["gat_w"][:], w["gat_src"][:], w["gat_dst"][:], w["gat_b_gat"][:], w["gat_ln_gamma"][:], w["gat_ln_beta"][:], scores)
        l3_experts(t, scores, w["e3_w1"], w["e3_w2"], w["e3_b2"])
        with t.stage("sent") as (block, sent):
            @block.sync
            def _(sp):
                sp.dma_start(out, t.h[:]).then_inc(sent, 16)
                sp.wait_ge(sent, 16)


FNO_INPUTS = ["p_w", "p_b", "fw", "w1_w", "w1_b", "w2_w", "w2_b", "q1_w", "q1_b", "q2_w", "q2_b"]


def kernel(**inputs):
    import concourse.bacc as bacc
    from concourse.bass_utils import run_bass_kernel_spmd

    inp = {k: np.asarray(v) for k, v in inputs.items()}
    nc = bacc.Bacc("TRN2", target_bir_lowering=False, num_devices=1)
    arrays = {}

    def dram(prefix, group):
        aps = {}
        for k, a in group.items():
            arrays[prefix + k] = a
            aps[k] = nc.dram_tensor(prefix + k, a.shape, mybir.dt.from_np(a.dtype), kind="ExternalInput").ap()
        return aps

    const = dram("c_", shape_constants())
    fno_in = dram("t_", {**fno_constants(), **fno_layout(inp["x"], *[inp["L0_tok_" + k] for k in FNO_INPUTS])})
    weights = dram("w_", tower_layout(inp))
    edges = dram("", {"edges": edge_layout(inp["L3_ffn_edge_index"])})["edges"]
    out = nc.dram_tensor("out", (P, TILES, D), F32, kind="ExternalOutput").ap()
    vit_tower(nc, const, fno_in, weights, edges, out)
    r = run_bass_kernel_spmd(nc, [arrays], core_ids=[0])
    return np.ascontiguousarray(np.asarray(r.results[0]["out"]).transpose(1, 0, 2)).reshape(NB, S, D)
```
